# Optimizing a Trainium2 kernel written in Bass

```python
import numpy as np
import jax
import jax.numpy as jnp

def _softmax(x, axis=-1):
    return jax.nn.softmax(x, axis=axis)

def _gelu(x):
    return jax.nn.gelu(x, approximate=True)

def _silu(x):
    return jax.nn.silu(x)

def _sigmoid(x):
    return jax.nn.sigmoid(x)

def _layernorm(x, axis=-1, eps=1e-05):
    m = jnp.mean(x, axis=axis, keepdims=True)
    v = jnp.var(x, axis=axis, keepdims=True)
    return (x - m) / jnp.sqrt(v + eps)

def _scatter_add(tgt, idx, src, axis=0):
    return tgt.at[idx].add(src)

def _segment_sum(src, seg, n):
    return jax.ops.segment_sum(src, seg, n)
kernel_name = 'mk_seq_postln_d1_jaxref_r4_a01e9a'

def setup_inputs(seed: int=0):
    np.random.seed(seed)
    _w = jnp.asarray

    def _L0_attn_setup():
        import jax, jax.numpy as jnp
        import numpy as np
        from jax import lax
        B, S, D = (8, 256, 256)
        DH = D // 2
        H = 8
        DK = DH // H
        DFF = 4 * D
        ALPHA, BETA = (0.1, 0.1)
        EPS = 1e-05
        PARAM_SPECS = [('wq1', (DH, DH)), ('bq1', (DH,)), ('wk1', (DH, DH)), ('bk1', (DH,)), ('wv1', (DH, DH)), ('bv1', (DH,)), ('wo1', (DH, DH)), ('bo1', (DH,)), ('wq2', (DH, DH)), ('bq2', (DH,)), ('wk2', (DH, DH)), ('bk2', (DH,)), ('wv2', (DH, DH)), ('bv2', (DH,)), ('wo2', (DH, DH)), ('bo2', (DH,)), ('g1', (DH,)), ('be1', (DH,)), ('g2', (DH,)), ('be2', (DH,)), ('w_ff1', (DFF, D)), ('b_ff1', (DFF,)), ('w_ff2', (D, DFF)), ('b_ff2', (D,)), ('g_ff', (D,)), ('be_ff', (D,))]

        def layernorm(x, g, b):
            m = jnp.mean(x, axis=-1, keepdims=True)
            v = jnp.mean(jnp.square(x - m), axis=-1, keepdims=True)
            return (x - m) * lax.rsqrt(v + EPS) * g + b

        def mha(xin, wq, bq, wk, bk, wv, bv, wo, bo):
            b, s, _ = xin.shape
            q = (xin @ wq.T + bq).reshape(b, s, H, DK)
            k = (xin @ wk.T + bk).reshape(b, s, H, DK)
            v = (xin @ wv.T + bv).reshape(b, s, H, DK)
            scores = jnp.einsum('bshd,bthd->bhst', q, k) * (1.0 / np.sqrt(DK).astype(np.float32))
            a = jax.nn.softmax(scores, axis=-1)
            o = jnp.einsum('bhst,bthd->bshd', a, v).reshape(b, s, DH)
            return o @ wo.T + bo

        def holt(x, alpha, beta):
            x0 = x[:, 0]

            def step(carry, xt):
                level, trend = carry
                nl = alpha * xt + (1.0 - alpha) * (level + trend)
                nt = beta * (nl - level) + (1.0 - beta) * trend
                return ((nl, nt), nl)
            _, lv = lax.scan(step, (x0, jnp.zeros_like(x0)), jnp.swapaxes(x[:, 1:], 0, 1))
            return jnp.concatenate([x0[:, None], jnp.swapaxes(lv, 0, 1)], axis=1)
        key = jax.random.key(seed)
        inp = {'x': jax.random.normal(jax.random.fold_in(key, 0), (B, S, D), jnp.float32)}
        for i, (name, shape) in enumerate(PARAM_SPECS):
            k = jax.random.fold_in(key, i + 1)
            if name.startswith('g'):
                inp[name] = jnp.ones(shape, jnp.float32)
            elif name.startswith('b'):
                inp[name] = jnp.zeros(shape, jnp.float32)
            else:
                inp[name] = jax.random.normal(k, shape, jnp.float32) * 0.02
        return inp
    _L0_attn_in = _L0_attn_setup()

    def _L0_ffn_setup():
        import jax, jax.numpy as jnp
        import numpy as np
        E = 16
        K = 4
        NG = 4
        TG = 2
        SCALE = 2.5
        NORM_TOPK = True
        H = 256
        I = 128
        SH_I = I * 2
        B, S = (2, 512)
        key = jax.random.key(seed)
        ks = jax.random.split(key, 9)

        def w(k, shape, fan_in):
            return jax.random.normal(k, shape, jnp.float32) * (1.0 / np.sqrt(fan_in))
        return {'hidden_states': jax.random.normal(ks[0], (B, S, H), jnp.float32), 'gate_w': w(ks[1], (E, H), H), 'gate_bias': jnp.zeros((E,), jnp.float32), 'Wg': w(ks[2], (E, I, H), H), 'Wu': w(ks[3], (E, I, H), H), 'Wd': w(ks[4], (E, H, I), I), 'Ws_g': w(ks[5], (SH_I, H), H), 'Ws_u': w(ks[6], (SH_I, H), H), 'Ws_d': w(ks[7], (H, SH_I), SH_I)}
    _L0_ffn_in = _L0_ffn_setup()
    _d = {'L0_attn_x': _L0_attn_in['x'], 'L0_attn_wq1': _L0_attn_in['wq1'], 'L0_attn_bq1': _L0_attn_in['bq1'], 'L0_attn_wk1': _L0_attn_in['wk1'], 'L0_attn_bk1': _L0_attn_in['bk1'], 'L0_attn_wv1': _L0_attn_in['wv1'], 'L0_attn_bv1': _L0_attn_in['bv1'], 'L0_attn_wo1': _L0_attn_in['wo1'], 'L0_attn_bo1': _L0_attn_in['bo1'], 'L0_attn_wq2': _L0_attn_in['wq2'], 'L0_attn_bq2': _L0_attn_in['bq2'], 'L0_attn_wk2': _L0_attn_in['wk2'], 'L0_attn_bk2': _L0_attn_in['bk2'], 'L0_attn_wv2': _L0_attn_in['wv2'], 'L0_attn_bv2': _L0_attn_in['bv2'], 'L0_attn_wo2': _L0_attn_in['wo2'], 'L0_attn_bo2': _L0_attn_in['bo2'], 'L0_attn_g1': _L0_attn_in['g1'], 'L0_attn_be1': _L0_attn_in['be1'], 'L0_attn_g2': _L0_attn_in['g2'], 'L0_attn_be2': _L0_attn_in['be2'], 'L0_attn_w_ff1': _L0_attn_in['w_ff1'], 'L0_attn_b_ff1': _L0_attn_in['b_ff1'], 'L0_attn_w_ff2': _L0_attn_in['w_ff2'], 'L0_attn_b_ff2': _L0_attn_in['b_ff2'], 'L0_attn_g_ff': _L0_attn_in['g_ff'], 'L0_attn_be_ff': _L0_attn_in['be_ff'], 'L0_ffn_gate_w': _L0_ffn_in['gate_w'], 'L0_ffn_gate_bias': _L0_ffn_in['gate_bias'], 'L0_ffn_Wg': _L0_ffn_in['Wg'], 'L0_ffn_Wu': _L0_ffn_in['Wu'], 'L0_ffn_Wd': _L0_ffn_in['Wd'], 'L0_ffn_Ws_g': _L0_ffn_in['Ws_g'], 'L0_ffn_Ws_u': _L0_ffn_in['Ws_u'], 'L0_ffn_Ws_d': _L0_ffn_in['Ws_d']}
    _x0 = _d['L0_attn_x']
    _d['L0_attn_x'] = jax.random.normal(jax.random.fold_in(jax.random.key(seed), 1), (4, 2048, 256), dtype=_x0.dtype)
    del _x0
    return _d

def reference(L0_attn_x, L0_attn_wq1, L0_attn_bq1, L0_attn_wk1, L0_attn_bk1, L0_attn_wv1, L0_attn_bv1, L0_attn_wo1, L0_attn_bo1, L0_attn_wq2, L0_attn_bq2, L0_attn_wk2, L0_attn_bk2, L0_attn_wv2, L0_attn_bv2, L0_attn_wo2, L0_attn_bo2, L0_attn_g1, L0_attn_be1, L0_attn_g2, L0_attn_be2, L0_attn_w_ff1, L0_attn_b_ff1, L0_attn_w_ff2, L0_attn_b_ff2, L0_attn_g_ff, L0_attn_be_ff, L0_ffn_gate_w, L0_ffn_gate_bias, L0_ffn_Wg, L0_ffn_Wu, L0_ffn_Wd, L0_ffn_Ws_g, L0_ffn_Ws_u, L0_ffn_Ws_d):

    def _L0_attn_ref(x, wq1, bq1, wk1, bk1, wv1, bv1, wo1, bo1, wq2, bq2, wk2, bk2, wv2, bv2, wo2, bo2, g1, be1, g2, be2, w_ff1, b_ff1, w_ff2, b_ff2, g_ff, be_ff):
        import jax, jax.numpy as jnp
        import numpy as np
        from jax import lax
        B, S, D = (8, 256, 256)
        DH = D // 2
        H = 8
        DK = DH // H
        DFF = 4 * D
        ALPHA, BETA = (0.1, 0.1)
        EPS = 1e-05
        PARAM_SPECS = [('wq1', (DH, DH)), ('bq1', (DH,)), ('wk1', (DH, DH)), ('bk1', (DH,)), ('wv1', (DH, DH)), ('bv1', (DH,)), ('wo1', (DH, DH)), ('bo1', (DH,)), ('wq2', (DH, DH)), ('bq2', (DH,)), ('wk2', (DH, DH)), ('bk2', (DH,)), ('wv2', (DH, DH)), ('bv2', (DH,)), ('wo2', (DH, DH)), ('bo2', (DH,)), ('g1', (DH,)), ('be1', (DH,)), ('g2', (DH,)), ('be2', (DH,)), ('w_ff1', (DFF, D)), ('b_ff1', (DFF,)), ('w_ff2', (D, DFF)), ('b_ff2', (D,)), ('g_ff', (D,)), ('be_ff', (D,))]

        def layernorm(x, g, b):
            m = jnp.mean(x, axis=-1, keepdims=True)
            v = jnp.mean(jnp.square(x - m), axis=-1, keepdims=True)
            return (x - m) * lax.rsqrt(v + EPS) * g + b

        def mha(xin, wq, bq, wk, bk, wv, bv, wo, bo):
            b, s, _ = xin.shape
            q = (xin @ wq.T + bq).reshape(b, s, H, DK)
            k = (xin @ wk.T + bk).reshape(b, s, H, DK)
            v = (xin @ wv.T + bv).reshape(b, s, H, DK)
            scores = jnp.einsum('bshd,bthd->bhst', q, k) * (1.0 / np.sqrt(DK).astype(np.float32))
            a = jax.nn.softmax(scores, axis=-1)
            o = jnp.einsum('bhst,bthd->bshd', a, v).reshape(b, s, DH)
            return o @ wo.T + bo

        def holt(x, alpha, beta):
            x0 = x[:, 0]

            def step(carry, xt):
                level, trend = carry
                nl = alpha * xt + (1.0 - alpha) * (level + trend)
                nt = beta * (nl - level) + (1.0 - beta) * trend
                return ((nl, nt), nl)
            _, lv = lax.scan(step, (x0, jnp.zeros_like(x0)), jnp.swapaxes(x[:, 1:], 0, 1))
            return jnp.concatenate([x0[:, None], jnp.swapaxes(lv, 0, 1)], axis=1)
        xh = x[:, :, :DH]
        x1 = layernorm(xh + mha(xh, wq1, bq1, wk1, bk1, wv1, bv1, wo1, bo1), g1, be1)
        xs = holt(x, ALPHA, BETA)
        xsh = xs[:, :, :DH]
        x2 = layernorm(xsh + mha(xsh, wq2, bq2, wk2, bk2, wv2, bv2, wo2, bo2), g2, be2)
        y = jnp.concatenate([x1, x2], axis=-1)
        y_ff = jax.nn.relu(y @ w_ff1.T + b_ff1) @ w_ff2.T + b_ff2
        return layernorm(y + y_ff, g_ff, be_ff)

    def _L0_ffn_ref(hidden_states, gate_w, gate_bias, Wg, Wu, Wd, Ws_g, Ws_u, Ws_d):
        import jax, jax.numpy as jnp
        import numpy as np
        E = 16
        K = 4
        NG = 4
        TG = 2
        SCALE = 2.5
        NORM_TOPK = True
        H = 256
        I = 128
        SH_I = I * 2
        B, S = (2, 512)
        x = hidden_states
        b, s, h = x.shape
        n = b * s
        xf = x.reshape(n, h)
        logits = xf @ gate_w.T
        scores = jax.nn.sigmoid(logits)
        sfc = scores + gate_bias
        epg = E // NG
        grp = sfc.reshape(n, NG, epg)
        g_scores = jax.lax.top_k(grp, 2)[0].sum(-1)
        _, gidx = jax.lax.top_k(g_scores, TG)
        gmask = jax.nn.one_hot(gidx, NG, dtype=sfc.dtype).sum(1)
        emask = jnp.repeat(gmask, epg, axis=1)
        masked = jnp.where(emask > 0, sfc, -jnp.inf)
        _, topk_idx = jax.lax.top_k(masked, K)
        topk_w = jnp.take_along_axis(scores, topk_idx, axis=1)
        if K > 1 and NORM_TOPK:
            topk_w = topk_w / (topk_w.sum(-1, keepdims=True) + 1e-20)
        topk_w = topk_w * SCALE
        cw = (jax.nn.one_hot(topk_idx, E, dtype=topk_w.dtype) * topk_w[..., None]).sum(1)
        hg = jnp.einsum('nh,eih->nei', xf, Wg)
        hu = jnp.einsum('nh,eih->nei', xf, Wu)
        act = jax.nn.silu(hg) * hu
        y = jnp.einsum('nei,ne,ehi->nh', act, cw, Wd)
        shared = jax.nn.silu(xf @ Ws_g.T) * (xf @ Ws_u.T) @ Ws_d.T
        y = y + shared
        return (x + y.reshape(b, s, h)).astype(hidden_states.dtype)
    x = L0_attn_x
    x = _layernorm(x + _L0_attn_ref(x, L0_attn_wq1, L0_attn_bq1, L0_attn_wk1, L0_attn_bk1, L0_attn_wv1, L0_attn_bv1, L0_attn_wo1, L0_attn_bo1, L0_attn_wq2, L0_attn_bq2, L0_attn_wk2, L0_attn_bk2, L0_attn_wv2, L0_attn_bv2, L0_attn_wo2, L0_attn_bo2, L0_attn_g1, L0_attn_be1, L0_attn_g2, L0_attn_be2, L0_attn_w_ff1, L0_attn_b_ff1, L0_attn_w_ff2, L0_attn_b_ff2, L0_attn_g_ff, L0_attn_be_ff), axis=-1)
    x = _layernorm(x + _L0_ffn_ref(x, L0_ffn_gate_w, L0_ffn_gate_bias, L0_ffn_Wg, L0_ffn_Wu, L0_ffn_Wd, L0_ffn_Ws_g, L0_ffn_Ws_u, L0_ffn_Ws_d), axis=-1)
    return x

_drawn_inputs = setup_inputs


def setup_inputs(seed=0):
    import zlib

    import numpy as np

    out = dict(_drawn_inputs(seed))
    spreads = {'L0_attn_bq1': (0.0, 0.8),
     'L0_attn_bk1': (0.0, 0.8),
     'L0_attn_bv1': (0.0, 0.1),
     'L0_attn_bo1': (0.0, 0.1),
     'L0_attn_bq2': (0.0, 0.8),
     'L0_attn_bk2': (0.0, 0.8),
     'L0_attn_bv2': (0.0, 0.1),
     'L0_attn_bo2': (0.0, 0.1),
     'L0_attn_g1': (1.0, 0.2),
     'L0_attn_be1': (0.0, 0.1),
     'L0_attn_g2': (1.0, 0.2),
     'L0_attn_be2': (0.0, 0.1),
     'L0_attn_b_ff1': (0.0, 0.1),
     'L0_attn_b_ff2': (0.0, 0.1),
     'L0_attn_g_ff': (1.0, 0.2),
     'L0_attn_be_ff': (0.0, 0.1),
     'L0_ffn_gate_bias': (0.0, 0.1)}
    factors = {'L0_attn_wq1': 8.0,
     'L0_attn_wk1': 8.0,
     'L0_attn_wv1': 8.0,
     'L0_attn_wq2': 8.0,
     'L0_attn_wk2': 8.0,
     'L0_attn_wv2': 4.414}
    for name, (base, spread) in spreads.items():
        noise = np.random.default_rng([zlib.crc32(name.encode()), seed]).standard_normal(out[name].shape)
        drawn = base * np.exp(spread * noise) if base else spread * noise
        out[name] = jnp.asarray(drawn.astype(out[name].dtype))
    for name, factor in factors.items():
        out[name] = (out[name] * factor).astype(out[name].dtype)
    return out
```

```python
import concourse.bass as bass
from concourse import mybir
from contextlib import ExitStack

F32 = mybir.dt.float32
BF16 = mybir.dt.bfloat16
ALU = mybir.AluOpType
ACT = mybir.ActivationFunctionType
AX = mybir.AxisListType

B, S, D = 4, 2048, 256
DH = D // 2
H, DK = 8, 16
T = 128
C = 512
NCH = S // C
NT = S // T
TC = C // T
G = 4
PAIRS = 2 * B
ALPHA, BETA, EPS = 0.1, 0.1, 1e-5


PERIODS = 2 * NCH
STEPS = NT
RING = 3


def extras(p, k):
    out = []
    if k == 1:
        out.append(("max_rows",))
    if k == 2:
        out.append(("o_tok",))
    if (p - 1) % PERIODS >= NCH:
        if k == 4:
            out.append(("o_feat",))
        if k == 6:
            out.append(("project",))
    if p in (2, 3):
        if k in (3, 5, 8, 10):
            i = (p - 2) * 4 + (3, 5, 8, 10).index(k)
            out.append(("qk", i % 2, i // 2))
        if k in (12, 13, 14) and (p, k) != (3, 14):
            i = (p - 2) * 3 + k - 12
            out.append(("v", (0, 4, 8, 12, 14)[i], (4, 4, 4, 2, 2)[i]))
    return out


def ring_jobs():
    at, n = {}, 0
    for p in range(PERIODS):
        for k in range(STEPS):
            for h in range(G):
                at[p, k, "max", h] = n
                n += 1
            for e in extras(p, k):
                at[(p, k) + e] = n
                n += 1
    return at, n


JOB, JOBS = ring_jobs()
assert JOBS % RING == 0
RUN_IN = ([("qk", w, c) for c in range(NCH) for w in range(2)] + [("v", t, 4) for t in range(0, NT, 4)]
          + [("max", 0, k, h) for k in range(STEPS) for h in range(G)] + [("max_rows",)]
          + [("max", 1, k, h) for k in range(STEPS) for h in range(G)])
R0 = len(RUN_IN)
Q_PART = (0, 0, 1, 0, 1, 2)
K_PART = (0, 1, 0, 2, 1, 0)
STACK = 2 * len(Q_PART) * G
COPIES = 4
ROWS = DK * len(Q_PART)


def attention(nc, x_tok, x_feat, holt_in, holt_state, holt_out, holt_carry, x0_rows,
              w_pairs, bias_qk, bias_v, bias_o, identity, xT_pairs, xN_pairs, z_pairs):
    with ExitStack() as ctx:
        sb = lambda name, shape, dt=F32: ctx.enter_context(nc.sbuf_tensor(name, shape, dt))
        sem = lambda name: ctx.enter_context(nc.semaphore(name))
        ks = [sb(f"k_rows{g}", [128, G, S], BF16) for g in range(2)]
        qs = [sb("q_rows0", [128, G, S], BF16)]
        qk_part = [[sb(f"{x}_part{i}", [128, S], BF16) for i in range(3)] for x in "qk"]
        va = sb("v_ones", [T, NT, H, 2 * DK])
        vs = sb("v_stage", [T, NT, DH])
        xT = sb("x_feat", [DH, S])
        w = sb("w_qkv", [DH, 3 * DH])
        wo = sb("w_o", [DH, DH])
        bqk = sb("b_qk", [DH, 2])
        bv = sb("b_v", [T, DH])
        bo = sb("b_o", [T, DH])
        ident = sb("ident", [128, 128])
        qk_f = [sb(f"qk_f{i}", [DH, C]) for i in range(2)]
        rest = sb("qk_rest", [DH, C])
        mpart = [sb(f"max_part{i}", [T, G * TC, NCH]) for i in range(2)]
        mneg = sb("max_neg", [T, G * TC])
        mrow = sb("max_row", [G * TC, 2, T], BF16)
        max_scratch = nc.dram_tensor("max_scratch", [2, G * TC, T], BF16, kind="Internal").ap()
        o_raw = sb("o_raw", [T, C])
        o_tok = sb("o_tok", [T, NT, DH])
        with ExitStack() as early:
            hb = lambda name, shape: early.enter_context(nc.sbuf_tensor(name, shape, F32))
            hx = hb("holt_x", [T, NT, B, DH])
            lin = hb("holt_lin", [T, T])
            lstate = hb("holt_lstate", [2 * NT, NT, T])
            lout = hb("holt_lout", [T, NT, 2 * NT])
            carry = hb("holt_carry", [2, 2 * NT])
            first = hb("holt_first", [2, B * DH])
            states = hb("holt_states", [2 * NT, B * DH])
            level = hb("holt_level", [T, 2, B * DH])
            level_T = hb("holt_level_T", [DH, 2, B, C])
        qs.append(sb("q_rows1", [128, G, S], BF16))
        prob = [sb(f"prob{i}", [T, G, C]) for i in range(2)]
        o_rec = sb("o_rec", [T, TC, G])
        o_feat = sb("o_feat", [DH, C])
        res = [sb(f"res{i}", [T, TC, DH]) for i in range(2)]
        res_b = sb("res_b", [T, TC, DH])
        z = [sb(f"z{i}", [T, TC, DH]) for i in range(2)]

        p_exp = [ctx.enter_context(nc.psum_tensor(f"p_exp{i}", [T, 2, C], F32)) for i in range(2)]
        p_ring = [ctx.enter_context(nc.psum_tensor(f"p_ring{i}", [128, C], F32)) for i in range(RING)]
        p_av = ctx.enter_context(nc.psum_tensor("p_av", [128, C], F32))
        p_level, p_turned, p_states = p_exp[0], p_exp[1], p_av[0:2 * NT, :]

        once = sem("once_loaded")
        holt_loaded, copied = sem("holt_loaded"), sem("copied")
        states_summed, states_set = sem("states_summed"), sem("states_set")
        level_made, level_out = sem("level_made"), sem("level_out")
        turned_made, turned_out = sem("turned_made"), sem("turned_out")
        level_stored = [sem(f"level_stored{i}") for i in range(2)]
        turned_stored = [sem(f"turned_stored{i}") for i in range(2)]
        qkv_loaded, o_loaded = sem("qkv_loaded"), sem("o_loaded")
        ones_set = sem("ones_set")
        ring_full, ring_read = sem("ring_full"), sem("ring_read")
        qk_ready, parts_ready, stacked = sem("qk_ready"), sem("parts_ready"), sem("stacked")
        split_step = sem("split_step")
        pool_passed, sp_passed = sem("pool_passed"), sem("sp_passed")
        v_copied = sem("v_copied")
        max_neg, max_high = sem("max_neg"), sem("max_high")
        rows_out, rows_stored = sem("rows_out"), sem("rows_stored")
        scored, exped, summed = sem("scored"), sem("exped"), sem("summed")
        o_raw_ready, o_rec_ready = sem("o_raw_ready"), sem("o_rec_ready")
        res_loaded, res_ready = sem("res_loaded"), sem("res_ready")
        z_stored = [sem(f"z_stored{i}") for i in range(2)]
        block = ctx.enter_context(nc.Block())

        ring_of = lambda n, job: n * JOBS + R0 + job
        step_of = lambda n, p, k: n * PERIODS * STEPS + p * STEPS + k
        finishes = lambda p: (p - 1) % PERIODS >= NCH
        FIN = [p for p in range(PERIODS) if finishes(p)]

        def stack_rows(queue, x, g):
            rows, parts = ((qs[g], Q_PART), (ks[g], K_PART))[x]
            for j, i in enumerate(parts):
                for h in range(G):
                    src = (g * G + h) * DK
                    queue.dma_start(rows[j * DK:(j + 1) * DK, h, :], qk_part[x][i][src:src + DK, :]
                                    ).then_inc(stacked, 16)

        @block.sync
        def _(sp):
            def load_qkv(n, x=None):
                sp.dma_start(w[:, :], w_pairs[n, :, 0:3 * DH]).then_inc(qkv_loaded, 16)
                sp.dma_start(bqk[:, :], bias_qk[n, :, :]).then_inc(qkv_loaded, 16)
                sp.dma_start(bv[:, :], bias_v[n, :, :]).then_inc(qkv_loaded, 16)
                sp.dma_start(xT[:, :], xT_pairs[n, :, :] if x is None else x).then_inc(qkv_loaded, 16)

            def load_o(n):
                sp.dma_start(wo[:, :], w_pairs[n, :, 3 * DH:4 * DH]).then_inc(o_loaded, 16)
                sp.dma_start(bo[:, :], bias_o[n, :, :]).then_inc(o_loaded, 16)

            def stack(g):
                for x in range(2):
                    stack_rows(sp, x, g)

            def store_rows(n, u, job):
                sp.wait_ge(ring_read, ring_of(n, job) + 1)
                g, c = u // NCH % 2, u % NCH
                sp.dma_start(max_scratch.rearrange("i r s -> r i s"), mrow[:, :, :]).then_inc(rows_out, 16)
                sp.wait_ge(rows_out, 16 * (n * PERIODS + u + 1))
                sp.dma_start(qs[g][ROWS:ROWS + 2, :, c * C:(c + 1) * C],
                             max_scratch.rearrange("i (h t) s -> i h (t s)", h=G)).then_inc(rows_stored, 16)

            def load_res(n, i, pair, c, f):
                sp.wait_ge(res_ready, n * len(FIN) + f + 1)
                sp.dma_start(res[i][:, :, :], xN_pairs[pair, c * C:(c + 1) * C, :].rearrange("(t p) f -> p t f", p=T)
                             ).then_inc(res_loaded, 16)

            def store_z(n, i, pair, c, job):
                sp.wait_ge(ring_read, ring_of(n, job) + 1)
                sp.dma_start(z_pairs[pair, c * C:(c + 1) * C, :].rearrange("(t p) f -> p t f", p=T),
                             z[i][:, :, :]).then_inc(z_stored[i], 16)

            for i in range(2):
                sp.sem_inc(z_stored[i], 16)
            sp.sem_inc(res_ready, 2)
            sp.dma_start(ident[:, :], identity).then_inc(once, 16)
            load_qkv(0, x_feat[0, :, :])
            load_o(0)
            for dst, src in [(lout[:, :, :], holt_out), (carry[:, :], holt_carry), (first[:, :], x0_rows),
                             (lin[:, :], holt_in), (lstate[:, :, :], holt_state)] + [
                                 (hx[:, :, b, :], x_tok[b, :, 0:DH].rearrange("(c t) f -> t c f", t=T)) for b in range(B)]:
                sp.dma_start(dst, src).then_inc(holt_loaded, 16)
            sp.wait_ge(ones_set, 4)
            sp.wait_ge(parts_ready, 2 * NCH)
            stack_rows(sp, 0, 0)
            store_rows(0, 0, RUN_IN.index(("max_rows",)) - R0)
            sp.wait_ge(copied, 16 * COPIES)
            for i in range(2):
                sp.wait_ge(level_stored[i], 16 * NT // 2)
                sp.wait_ge(turned_stored[i], 16 * NCH // 2)

            def period(n, p):
                if finishes(p):
                    f = FIN.index(p)
                    load_res(n, f % 2, n if p == 0 else n + 1, (p - 1) % NCH, f)
                if p == 0:
                    sp.wait_ge(ring_full, ring_of(n, 0))
                    stack(1)
                if p == 1:
                    sp.wait_ge(ring_read, ring_of(n, JOB[1, 0, "max", 0]))
                    load_qkv(n + 1)
                    load_o(n)
                store_rows(n, p + 1, JOB[p, 1, "max_rows"])
                if p == NCH:
                    sp.wait_ge(scored, 2 * step_of(n, NCH, 0))
                    sp.sem_inc(sp_passed, 1)
                    sp.wait_ge(parts_ready, 2 * NCH * n + 4 * NCH)
                    stack(0)
                if finishes(p):
                    store_z(n, f % 2, n if p == 0 else n + 1, (p - 1) % NCH, JOB[p, 6, "project"])

            with sp.Fori(0, PAIRS) as n:
                for p in range(PERIODS):
                    period(n, p)
            load_res(PAIRS, 0, PAIRS, NCH - 1, 0)
            store_z(PAIRS, 0, PAIRS, NCH - 1, 2)
            sp.wait_ge(z_stored[0], 16 * (2 * PAIRS + 2))
            sp.wait_ge(z_stored[1], 16 * (2 * PAIRS + 1))
            sp.wait_ge(stacked, 16 * STACK * (2 * PAIRS + 1))
            sp.wait_ge(rows_stored, 16 * (PERIODS * PAIRS + 1))
            sp.wait_ge(qkv_loaded, 64 * (PAIRS + 1))

        @block.tensor
        def _(pe):
            def ring_bank(n, job):
                idx = ring_of(n, job)
                if not isinstance(n, int) or idx >= RING:
                    pe.wait_ge(ring_read, idx - RING + 1)
                return p_ring[(R0 + job) % RING]

            def max_scores(n, job, g, c, k, h):
                bank = ring_bank(n, job)
                q0, k0 = c * C + (k // NCH) * T, (k % NCH) * C
                nc.tensor.matmul(bank[:, :], qs[g][0:ROWS, h, q0:q0 + T], ks[g][0:ROWS, h, k0:k0 + C],
                                 start=True, stop=True).then_inc(ring_full, 1)

            def max_rows(n, job, done):
                bank = ring_bank(n, job)
                pe.wait_ge(max_neg, done)
                nc.tensor.transpose(bank[0:G * TC, 0:T], mneg[:, :], ident[:, :]).then_inc(ring_full, 1)

            def project_qk(n, job, which, c):
                bank = ring_bank(n, job)
                nc.tensor.matmul(bank[:, :], w[:, which * DH:(which + 1) * DH], xT[:, c * C:(c + 1) * C],
                                 start=True, stop=True).then_inc(ring_full, 1)

            def project_v(n, job, t0, count):
                bank = ring_bank(n, job)
                for i in range(count):
                    last = nc.tensor.matmul(bank[:, i * DH:(i + 1) * DH], xT[:, (t0 + i) * T:(t0 + i + 1) * T],
                                            w[:, 2 * DH:3 * DH], start=True, stop=True)
                last.then_inc(ring_full, 1)

            def score(n, p, k, pair):
                g, c = p // NCH, p % NCH
                e = 2 * step_of(n, p, k) + pair
                if p or k:
                    pe.wait_ge(exped, e - 1)
                for i in range(2):
                    h = 2 * pair + i
                    last = nc.tensor.matmul(p_exp[pair][:, i, :], ks[g][0:ROWS + 2, h, k * T:(k + 1) * T],
                                            qs[g][0:ROWS + 2, h, c * C:(c + 1) * C], start=True, stop=True)
                last.then_inc(scored, 1)

            def weigh(n, p, k):
                pe.wait_ge(exped, 2 * step_of(n, p, k) + 2)
                if k == 0:
                    pe.wait_ge(o_raw_ready, n * PERIODS + p + 1)
                    if p % NCH == 0:
                        pe.wait_ge(v_copied, 2 * n + p // NCH + 1)
                for h in range(G):
                    last = nc.tensor.matmul(p_av[32 * h:32 * h + 2 * DK, :], va[:, k, p // NCH * G + h, :],
                                            prob[k % 2][:, h, :], start=(k == 0), stop=(k == STEPS - 1))
                last.then_inc(summed, 1)

            def outputs_to_tokens(n, job, done):
                bank = ring_bank(n, job)
                pe.wait_ge(o_raw_ready, done)
                for t in range(TC):
                    last = nc.tensor.transpose(bank[:, t * T:(t + 1) * T], o_raw[:, t * T:(t + 1) * T], ident[:, :])
                last.then_inc(ring_full, 1)

            def outputs_to_features(n, job, after, c):
                bank = ring_bank(n, job)
                pe.wait_ge(ring_read, ring_of(n, after) + 1)
                for t in range(TC):
                    last = nc.tensor.transpose(bank[:, t * T:(t + 1) * T], o_tok[:, c * TC + t, :], ident[:, :])
                last.then_inc(ring_full, 1)

            def project_out(n, job, after):
                bank = ring_bank(n, job)
                pe.wait_ge(ring_read, ring_of(n, after) + 1)
                for t in range(TC):
                    last = nc.tensor.matmul(bank[:, t * DH:(t + 1) * DH], o_feat[:, t * T:(t + 1) * T], wo[:, :],
                                            start=True, stop=True)
                last.then_inc(ring_full, 1)

            def sum_states():
                pe.wait_ge(holt_loaded, 9 * 16)
                nc.tensor.matmul(p_states, carry[:, :], first[:, :], start=True, stop=False)
                for c in range(NT - 1):
                    last = nc.tensor.matmul(p_states, lout[:, c, :], hx[:, c, :, :].rearrange("t b f -> t (b f)"),
                                            start=False, stop=(c == NT - 2))
                last.then_inc(states_summed, 1)

            def levels(c):
                pe.wait_ge(states_set, 1)
                if c >= 2:
                    pe.wait_ge(level_out, c - 1)
                nc.tensor.matmul(p_level[:, c % 2, :], lin[:, :], hx[:, c, :, :].rearrange("t b f -> t (b f)"),
                                 start=True, stop=False)
                nc.tensor.matmul(p_level[:, c % 2, :], lstate[:, c, :], states[:, :], start=False, stop=True
                                 ).then_inc(level_made, 1)

            def turn_levels(c):
                pe.wait_ge(level_out, c + 1)
                if c >= 2:
                    pe.wait_ge(turned_out, c - 1)
                for b in range(B):
                    last = nc.tensor.transpose(p_turned[:, c % 2, b * T:(b + 1) * T],
                                               level[:, c % 2, b * DH:(b + 1) * DH], ident[:, :])
                last.then_inc(turned_made, 1)

            pe.wait_ge(once, 16)
            pe.wait_ge(o_loaded, 32)
            pe.wait_ge(qkv_loaded, 64)
            for i, job in enumerate(RUN_IN):
                if job == ("max", 0, 0, 0):
                    sum_states()
                if job[0] == "qk":
                    project_qk(0, i - R0, job[1], job[2])
                elif job[0] == "v":
                    project_v(0, i - R0, job[1], job[2])
                elif job[0] == "max_rows":
                    max_rows(0, i - R0, 1)
                else:
                    if job == ("max", 0, 0, 0):
                        pe.wait_ge(stacked, 16 * STACK)
                    max_scores(0, i - R0, 0, job[1], job[2], job[3])
                    at = (job[1] * STEPS + job[2]) * G + job[3]
                    if at % 7 == 1 and at // 7 < NT:
                        levels(at // 7)
                    if at % 7 == 4 and at // 7 < NT:
                        turn_levels(at // 7)
            pe.wait_ge(level_out, NT)
            pe.wait_ge(turned_out, NT)

            def extra(n, p, k, e):
                job = JOB[(p, k) + e]
                if e[0] == "max_rows":
                    max_rows(n, job, n * PERIODS + p + 2)
                elif e[0] == "o_tok":
                    outputs_to_tokens(n, job, n * PERIODS + p + 1)
                elif e[0] == "o_feat":
                    outputs_to_features(n, job, JOB[p, 2, "o_tok"], (p - 1) % NCH)
                elif e[0] == "project":
                    if p == 5:
                        pe.wait_ge(o_loaded, 32 * n + 64)
                    project_out(n, job, JOB[p, 4, "o_feat"])
                elif e[0] == "qk":
                    if e[1:] == (0, 0):
                        pe.wait_ge(qkv_loaded, 64 * n + 128)
                    project_qk(n, job, e[1], e[2])
                else:
                    project_v(n, job, e[1], e[2])

            with pe.Fori(0, PAIRS) as n:
                for p in range(PERIODS):
                    u = p + 2
                    for k in range(STEPS):
                        if k == 0:
                            pe.wait_ge(rows_stored, 16 * (n * PERIODS + p + 1))
                            if u % NCH == 0:
                                pe.wait_ge(stacked, 16 * STACK * (2 * n + u // NCH + 1))
                        score(n, p, k, 0)
                        for h in range(2):
                            max_scores(n, JOB[p, k, "max", h], u // NCH % 2, u % NCH, k, h)
                        score(n, p, k, 1)
                        if k:
                            weigh(n, p, k - 1)
                        elif p:
                            weigh(n, p - 1, STEPS - 1)
                        for h in range(2, G):
                            max_scores(n, JOB[p, k, "max", h], u // NCH % 2, u % NCH, k, h)
                        for e in extras(p, k):
                            extra(n, p, k, e)
                weigh(n, PERIODS - 1, STEPS - 1)
            outputs_to_tokens(PAIRS, 0, PAIRS * PERIODS + 1)
            outputs_to_features(PAIRS, 1, 0, NCH - 1)
            project_out(PAIRS, 2, 1)

        @block.scalar
        def _(act):
            def take_outputs(n, done, job):
                act.wait_ge(summed, done)
                act.wait_ge(ring_full, job)
                nc.scalar.activation(o_raw[:, :], p_av[:, :], ACT.Copy).then_inc(o_raw_ready, 1)

            def take_levels(c):
                act.wait_ge(level_made, c + 1)
                if c >= 2:
                    act.wait_ge(level_stored[c % 2], 16 * (c // 2))
                    act.wait_ge(turned_made, c - 1)
                nc.scalar.activation(level[:, c % 2, :], p_level[:, c % 2, :], ACT.Copy).then_inc(level_out, 1)
                act.wait_ge(level_out, c + 1)
                act.dma_start(xN_pairs[1 + B:1 + 2 * B, c * T:(c + 1) * T, :].rearrange("b t f -> t b f"),
                              level[:, c % 2, :].rearrange("t (b f) -> t b f", b=B)).then_inc(level_stored[c % 2], 16)

            def take_turned(c):
                q = c // TC
                act.wait_ge(turned_made, c + 1)
                if q >= 2:
                    act.wait_ge(turned_stored[q % 2], 16 * (q // 2))
                nc.scalar.activation(level_T[:, q % 2, :, (c % TC) * T:(c % TC + 1) * T],
                                     p_turned[:, c % 2, :].rearrange("f (b t) -> f b t", b=B), ACT.Copy
                                     ).then_inc(turned_out, 1)
                if c % TC == TC - 1:
                    act.wait_ge(turned_out, c + 1)
                    act.dma_start(xT_pairs[B:2 * B, :, q * C:(q + 1) * C].rearrange("b f t -> f b t"),
                                  level_T[:, q % 2, :, :]).then_inc(turned_stored[q % 2], 16)

            act.wait_ge(ones_set, 4)
            act.wait_ge(parts_ready, 2 * NCH)
            stack_rows(act, 1, 0)
            for c in range(NT):
                take_levels(c)
                take_turned(c)
            for i in range(2):
                act.wait_ge(level_stored[i], 16 * NT // 2)
                act.wait_ge(turned_stored[i], 16 * NCH // 2)

            with act.Fori(0, PAIRS) as n:
                for p in range(PERIODS):
                    for k in range(STEPS):
                        for pair in range(2):
                            act.wait_ge(scored, 2 * step_of(n, p, k) + pair + 1)
                            if p or k >= 2:
                                act.wait_ge(summed, step_of(n, p, k) - 1)
                            nc.scalar.activation(prob[k % 2][:, 2 * pair:2 * pair + 2, :], p_exp[pair][:, :, :],
                                                 ACT.Exp, scale=1.0 / DK ** 0.5).then_inc(exped, 1)
                        if k == 0 and p:
                            take_outputs(n, step_of(n, p, 0), ring_of(n, JOB[p - 1, 2, "o_tok"]) + 1)
                take_outputs(n, step_of(n, PERIODS, 0), ring_of(n, JOB[PERIODS - 1, 2, "o_tok"]) + 1)

        @block.vector
        def _(dve):
            def full(n, job):
                dve.wait_ge(ring_full, ring_of(n, job) + 1)
                return p_ring[(R0 + job) % RING]

            def take_max(n, job, par, k, h):
                nc.vector.reduce_max(mpart[par][:, h * TC + k // NCH, k % NCH:k % NCH + 1], full(n, job)[:, :],
                                     AX.X).then_inc(ring_read, 1)

            def combine(n, job, par):
                dve.wait_ge(ring_read, ring_of(n, job))
                nc.vector.tensor_reduce(mneg[:, :], mpart[par][:, :, :], AX.X, ALU.max, negate=True
                                        ).then_inc(max_neg, 1)

            def split_rows(n, job, done):
                bank = full(n, job)
                if not isinstance(done, int) or done:
                    dve.wait_ge(rows_stored, 16 * done)
                nc.vector.tensor_copy(mrow[:, 0, :], bank[0:G * TC, 0:T]).then_inc(max_high, 1)
                dve.wait_ge(max_high, done + 1)
                nc.vector.tensor_tensor(mrow[:, 1, :], bank[0:G * TC, 0:T], mrow[:, 0, :], ALU.subtract
                                        ).then_inc(ring_read, 1)

            def take_qk(n, job, which, i, done):
                bank = full(n, job)
                if not isinstance(done, int) or done >= 2:
                    dve.wait_ge(parts_ready, done - 1)
                nc.vector.tensor_scalar(qk_f[i % 2][:, :], bank[:, :], bqk[:, which:which + 1], None, ALU.add
                                        ).then_inc(ring_read, 1)

            def take_v(n, job, t0, count):
                bank = full(n, job)
                nc.vector.tensor_tensor(vs[:, t0:t0 + count, :], bank[:, 0:count * DH].rearrange("p (t f) -> p t f", f=DH),
                                        bv[:, :].rearrange("p (o f) -> p o f", o=1).broadcast_to([T, count, DH]),
                                        ALU.add).then_inc(ring_read, 1)

            def normalise(n, job, g, c, done):
                bank = full(n, job)[:, :].rearrange("p (t h d) -> p t h d", t=TC, h=G)
                nc.vector.reciprocal(o_rec[:, :, :], bank[:, :, :, DK]).then_inc(o_rec_ready, 1)
                dve.wait_ge(o_rec_ready, done + 1)
                nc.vector.tensor_tensor(
                    o_tok[:, c * TC:(c + 1) * TC, g * G * DK:(g + 1) * G * DK].rearrange("p t (h d) -> p t h d", h=G),
                    bank[:, :, :, 0:DK], o_rec[:, :, :].rearrange("p t (h o) -> p t h o", o=1).broadcast_to([T, TC, G, DK]),
                    ALU.mult).then_inc(ring_read, 1)

            def take_features(n, job):
                nc.vector.tensor_copy(o_feat[:, :], full(n, job)[:, :]).then_inc(ring_read, 1)

            def add_residual(n, job, i, done, stores):
                bank = full(n, job)
                dve.wait_ge(res_ready, done + 3)
                dve.wait_ge(z_stored[i], 16 * stores)
                nc.vector.tensor_tensor(z[i][:, :, :], bank[:, :].rearrange("p (t f) -> p t f", t=TC), res_b[:, :, :],
                                        ALU.add).then_inc(ring_read, 1)

            def split(which, i, c):
                parts = qk_part[which]
                cols = slice(c * C, (c + 1) * C)
                dve.wait_ge(ring_read, i + 1)
                nc.vector.tensor_copy(parts[0][:, cols], qk_f[i % 2][:, :]).then_inc(split_step, 1)
                dve.wait_ge(split_step, 3 * i + 1)
                nc.vector.tensor_tensor(rest[:, :], qk_f[i % 2][:, :], parts[0][:, cols], ALU.subtract
                                        ).then_inc(split_step, 1)
                dve.wait_ge(split_step, 3 * i + 2)
                nc.vector.tensor_copy(parts[1][:, cols], rest[:, :]).then_inc(split_step, 1)
                dve.wait_ge(split_step, 3 * i + 3)
                nc.vector.tensor_tensor(parts[2][:, cols], rest[:, :], parts[1][:, cols], ALU.subtract
                                        ).then_inc(parts_ready, 1)
                dve.wait_ge(parts_ready, i + 1)

            dve.wait_ge(qkv_loaded, 64)
            for i, job in enumerate(RUN_IN):
                if job == ("max", 0, 0, 0):
                    dve.wait_ge(states_summed, 1)
                    nc.vector.tensor_copy(states[:, :], p_states).then_inc(states_set, 1)
                if job[0] == "qk":
                    take_qk(0, i - R0, job[1], i, i)
                    split(job[1], i, job[2])
                elif job[0] == "v":
                    take_v(0, i - R0, job[1], job[2])
                elif job[0] == "max":
                    take_max(0, i - R0, job[1], job[2], job[3])
                else:
                    split_rows(0, i - R0, 0)
                if job == ("max", 0, STEPS - 1, G - 1):
                    combine(0, i + 1 - R0, 0)

            def extra(n, p, k, e):
                job = JOB[(p, k) + e]
                if e[0] == "max_rows":
                    split_rows(n, job, n * PERIODS + p + 1)
                elif e[0] == "o_tok":
                    normalise(n, job, (p - 1) % PERIODS // NCH, (p - 1) % NCH, n * PERIODS + p)
                elif e[0] == "o_feat":
                    take_features(n, job)
                elif e[0] == "project":
                    f = FIN.index(p)
                    add_residual(n, job, f % 2, n * len(FIN) + f, n * 2 + f // 2 + 1)
                elif e[0] == "qk":
                    i = 2 * e[2] + e[1]
                    if i == 0:
                        dve.wait_ge(qkv_loaded, 64 * n + 128)
                    take_qk(n, job, e[1], i, 2 * NCH * n + 2 * NCH + i)
                else:
                    if e[1] == 0:
                        dve.wait_ge(v_copied, 2 * n + 2)
                    take_v(n, job, e[1], e[2])

            with dve.Fori(0, PAIRS) as n:
                for p in range(PERIODS):
                    for k in range(STEPS):
                        if k == 0:
                            combine(n, JOB[p, 0, "max", 0], (p + 1) % 2)
                        for h in range(G):
                            take_max(n, JOB[p, k, "max", h], p % 2, k, h)
                        for e in extras(p, k):
                            extra(n, p, k, e)
            normalise(PAIRS, 0, 1, NCH - 1, PAIRS * PERIODS)
            take_features(PAIRS, 1)
            add_residual(PAIRS, 2, 0, PAIRS * len(FIN), 2 * PAIRS + 1)

        @block.gpsimd
        def _(pool):
            def split(n, job, which, i, c, done):
                parts = qk_part[which]
                cols = slice(c * C, (c + 1) * C)
                pool.wait_ge(ring_read, ring_of(n, job) + 1)
                pool.sem_inc(pool_passed, 1)
                nc.gpsimd.tensor_copy(parts[0][:, cols], qk_f[i % 2][:, :]).then_inc(split_step, 1)
                pool.wait_ge(split_step, 3 * done + 1)
                nc.gpsimd.tensor_tensor(rest[:, :], qk_f[i % 2][:, :], parts[0][:, cols], ALU.subtract
                                        ).then_inc(split_step, 1)
                pool.wait_ge(split_step, 3 * done + 2)
                pool.sem_inc(pool_passed, 1)
                nc.gpsimd.tensor_copy(parts[1][:, cols], rest[:, :]).then_inc(split_step, 1)
                pool.wait_ge(split_step, 3 * done + 3)
                nc.gpsimd.tensor_tensor(parts[2][:, cols], rest[:, :], parts[1][:, cols], ALU.subtract
                                        ).then_inc(parts_ready, 1)
                pool.wait_ge(parts_ready, done + 1)

            def place_values(g, done):
                pool.sem_inc(pool_passed, 1)
                nc.gpsimd.tensor_copy(va[:, :, g * G:(g + 1) * G, 0:DK],
                                      vs[:, :, g * G * DK:(g + 1) * G * DK].rearrange("p t (h d) -> p t h d", h=G)
                                      ).then_inc(v_copied, 1)

            def bias_residual(i, done, loads, last):
                pool.wait_ge(res_loaded, 16 * (done + 1))
                pool.wait_ge(ring_read, last)
                pool.wait_ge(o_loaded, 32 * loads)
                nc.gpsimd.tensor_tensor(res_b[:, :, :], res[i][:, :, :],
                                        bo[:, :].rearrange("p (o f) -> p o f", o=1).broadcast_to([T, TC, DH]), ALU.add
                                        ).then_inc(res_ready, 1)

            fills = [(ks[0][ROWS:ROWS + 2, :, :], 1.0), (ks[1][ROWS:ROWS + 2, :, :], 1.0), (va[:, :, :, :], 1.0),
                     (o_tok[:, :, :], 0.0)]
            for i, (dst, value) in enumerate(fills):
                nc.gpsimd.memset(dst, value).then_inc(ones_set, 1)
                pool.wait_ge(ones_set, i + 1)
            nc.gpsimd.memset(o_raw[:, :], 1.0).then_inc(o_raw_ready, 1)
            pool.wait_ge(o_raw_ready, 1)
            copies = [(xT_pairs[0:B, :, :], x_feat), (xT_pairs[2 * B:2 * B + 1, :, :], x_feat[0:1, :, :]),
                      (xN_pairs[1:1 + B, :, :], x_tok[:, :, 0:DH]), (xN_pairs[0:1, :, :], x_tok[0:1, :, 0:DH])]
            assert len(copies) == COPIES
            for dst, src in copies:
                pool.dma_start(dst, src).then_inc(copied, 16)
            pool.wait_ge(ring_read, 2 * NCH + NT // 4)
            place_values(0, 0)

            def residual_of(n, p):
                f = FIN.index(p)
                before = JOB[FIN[f - 1], 6, "project"] - (JOBS if f == 0 else 0)
                bias_residual(f % 2, n * len(FIN) + f, n + 1 if p == 0 else n + 2, ring_of(n, before) + 1)

            with pool.Fori(0, PAIRS) as n:
                residual_of(n, 0)
                pool.wait_ge(o_raw_ready, n * PERIODS + 1)
                place_values(1, 2 * n + 1)
                pool.wait_ge(stacked, 16 * STACK * (2 * n + 2))
                for p in (2, 3):
                    for k in range(STEPS):
                        for e in extras(p, k):
                            if e[0] == "qk":
                                i = 2 * e[2] + e[1]
                                split(n, JOB[(p, k) + e], e[1], i, e[2], 2 * NCH * n + 2 * NCH + i)
                pool.wait_ge(summed, step_of(n, NCH, 0))
                place_values(0, 2 * n + 2)
                for p in FIN[1:]:
                    residual_of(n, p)
            residual_of(PAIRS, 0)


F32R = mybir.dt.float32r
CHUNKS = B * NCH
DFF, E, TOPK, NG, TOPG, ROUTED_SCALE = 1024, 16, 4, 4, 2, 2.5
EG = E // NG
NF = DFF // 128
NX = E + 2
UNITS = NF + NX
KC = D // 128
CW = 2
FIRST, LOOP_FIRST, LOOP_TURNS = -2, 1, 6
BIG = 3e38

SLOT = dict(f_turn=2, f_add=3, f_scale=4, f_norm=6,
            r_turn=10, r_add=11, r_scale=12, r_norm=12,
            s_add=13, s_scale=13, s_norm=13, h_turn=15, h_take=15, gate=17, gate_take=17, gate_exp=17,
            route_groups=17, route_experts=19, route_weights=22, cw_turn=24, cw_take=24,
            z_stats=16, z_scale=17, z_norm=20, y_turn=22, y_take=22)
TURNS = [("f", 0), ("f", 1), ("r", 0), ("r", 1), ("h", 0), ("h", 1), ("gate", 0), ("y", 0), ("y", 1), ("cw", 0)]
LAG = 2
V_LINKS = 55


class Period:

    def __init__(self, i, turn=None):
        self.i, self.turn = i, turn
        self.prev = i >= 1
        self.experts = i >= 0
        self.next = 0 <= i + 1 < CHUNKS
        self.next2 = i + 2 < CHUNKS
        self.units = (list(range(NF)) if self.next else []) + (list(range(NF, UNITS)) if self.experts else [])
        self.carried = self.prev and self.next
        self.carries = self.experts and self.next2
        self.jobs = [j for j in TURNS if {"f": self.prev, "y": self.next2}.get(j[0], self.next)]

    def at(self, table):
        if self.turn is None:
            return table(self.i)
        return self.turn * (table(self.i + 2) - table(self.i)) + table(self.i)

    def num(self, plus=0):
        return self.at(lambda i: i + plus)

    def ring(self, job, j=0):
        return self.at(turns_before) + self.jobs.index((job, j))

    def bank(self, job, j=0):
        return (turns_before(self.i) + self.jobs.index((job, j))) % 2

    def unit(self, u):
        return self.at(units_before) + self.units.index(u)

    def side(self, u):
        return (units_before(self.i) + self.units.index(u)) % 2


def turns_before(i):
    return sum(len(Period(j).jobs) for j in range(FIRST, i))


def units_before(i):
    return sum(len(Period(j).units) for j in range(FIRST, i))


def run_periods(engine, period, chain=None):
    for i in range(FIRST, LOOP_FIRST):
        period(Period(i))
    with engine.Fori(0, LOOP_TURNS) as turn:
        if chain is not None:
            chain.enter(turn)
        for i in range(LOOP_FIRST, LOOP_FIRST + 2):
            period(Period(i, turn))
        if chain is not None:
            chain.leave(LOOP_TURNS)
    for i in range(LOOP_FIRST + 2 * LOOP_TURNS, CHUNKS):
        period(Period(i))


class Count:

    def __init__(self, per_turn):
        self.n, self.per_turn, self.turn, self.start = 0, per_turn, None, 0

    def enter(self, turn):
        self.turn, self.start = turn, self.n

    def leave(self, turns):
        assert self.n - self.start == self.per_turn, (self.n - self.start, self.per_turn)
        self.turn, self.n = None, self.start + turns * self.per_turn

    def next(self):
        self.n += 1
        return self.n if self.turn is None else self.turn * self.per_turn + self.n


def experts(nc, x_tok, z_pairs, ff1, ff2, gate_t, exp_g, exp_u, exp_d, ff_bias1, ff_bias2, affine, gate_bias,
            lower, identity, out):
    x_rows = x_tok.rearrange("b s f -> (b s) f")
    z_rows = z_pairs.rearrange("n s f -> (n s) f")
    out_rows = out.rearrange("b s f -> (b s) f")
    cw_scratch = nc.dram_tensor("cw_scratch", [2, E, C], F32, kind="Internal").ap()
    with ExitStack() as ctx:
        sb = lambda name, shape, dt=F32: ctx.enter_context(nc.sbuf_tensor(name, shape, dt))
        sem = lambda name: ctx.enter_context(nc.semaphore(name))
        w1 = sb("w_ff1", [128, KC, DFF])
        w2 = sb("w_ff2", [128, NF, D])
        gw = [sb(f"w_gate{i}", [128, KC * E], F32R) for i in range(2)]
        wg = [sb(f"w_g{i}", [128, NX * D], F32R) for i in range(2)]
        wu = [sb(f"w_u{i}", [128, NX * D], F32R) for i in range(2)]
        wd = [sb(f"w_d{i}", [128, NX * D], F32R) for i in range(2)]
        b1 = sb("bias1", [128, NF])
        b2 = sb("bias2", [128, KC])
        aff = sb("affine", [T, 4, D])
        gb = sb("gate_b", [T, E])
        low = sb("lower", [T, E, E])
        low4 = sb("lower4", [T, NG, NG])
        ident = sb("ident2", [128, 128])
        power = sb("power", [T, 2 * TC])
        z = sb("z_in", [T, TC, D])
        yT = sb("y_feat", [128, KC, C])
        turned = sb("turned", [128, KC * C])
        x = sb("x_in", [T, TC * D])
        h = sb("h_tok", [T, 2, TC, D])
        fin = sb("final", [T, TC, D])
        hT = [[sb(f"h_feat{par}{i}", [128, KC, C], F32R) for i in range(2)] for par in range(2)]
        act_hi = [sb(f"act_hi{i}", [128, C], F32R) for i in range(2)]
        act_lo = [sb(f"act_lo{i}", [128, C], F32R) for i in range(2)]
        gated = [sb(f"gated{i}", [128, C]) for i in range(2)]
        cwb = sb("cw_all", [128, 2, CW, C])
        NORMS = "zrsf"
        stats = {k: sb(f"{k}_stats", [T, 2 * TC, 6]) for k in NORMS}
        mv = {k: sb(f"{k}_mean_var", [T, 2 * TC, 2]) for k in NORMS}
        scale = {k: sb(f"{k}_scale", [T, 2 * TC]) for k in NORMS}
        var_eps = {k: sb(f"{k}_var_eps", [T, 2 * TC]) for k in NORMS}
        logit = sb("logit", [T, TC * E])
        expo = sb("exp_neg", [T, TC * E])
        score = sb("score", [T, TC * E])
        biased = sb("biased", [T, TC * NG, EG])
        pair_sum = sb("pair_sums", [T, TC * NG, 6])
        gscore = sb("group_score", [T, TC, NG])
        gcmp = [sb(f"group_cmp{i}", [T, TC, NG, NG]) for i in range(2)]
        grank = sb("group_rank", [T, TC * NG])
        gpen = sb("group_penalty", [T, TC * NG])
        masked = sb("masked", [T, TC * NG, EG])
        erank = sb("expert_rank", [T, TC * E])
        wsel = sb("w_selected", [T, TC, E])
        wsum = sb("w_sum", [T, TC])
        cw = sb("cw_tok", [T, TC, E])
        cwT = sb("cw_feat", [E, C])
        ecmp = [b_[:, :].rearrange("p (t i j) -> p t i j", t=TC, i=E) for b_ in (turned, x)]

        p_unit = [ctx.enter_context(nc.psum_tensor(f"p_unit{i}", [128, 2, C], F32)) for i in range(2)]
        p_acc = ctx.enter_context(nc.psum_tensor("p_acc", [128, KC, C], F32))
        p_ring = [ctx.enter_context(nc.psum_tensor(f"p_turn{i}", [128, C], F32)) for i in range(2)]

        const_loaded, raw_loaded = sem("const_loaded"), [sem(f"raw_loaded{i}") for i in range(2)]
        hi_made, lo_made, power_set = sem("w_hi_made"), sem("w_lo_made"), sem("power_set")
        ring_full, ring_read = sem("turn_full"), sem("turn_read")
        up_done, silu_done, weighted, operand = sem("up_done"), sem("silu_done"), sem("weighted"), sem("operand")
        product_made, down_done, ff_taken, sum_taken = sem("product_made"), sem("down_done"), sem("ff_taken"), sem("sum_taken")
        z_loaded, x_loaded = sem("z_loaded"), sem("x_loaded")
        cw_ready, cw_stored = sem("cw_ready"), sem("cw_stored")
        cw_loaded = [sem(f"cw_loaded{i}") for i in range(2)]
        var_ready = {k: sem(f"{k}_var_ready") for k in NORMS}
        scale_ready = {k: sem(f"{k}_scale_ready") for k in NORMS}
        y_ready, h_ready, gate_exped = sem("y_ready"), sem("h_ready"), sem("gate_exped")
        f_ready, f_stored = sem("f_ready"), sem("f_stored")
        v_step = sem("v_step")
        v_passed, s_passed = sem("v_passed"), sem("s_passed")
        block = ctx.enter_context(nc.Block())

        STAGE = 2 * TC * D
        pieces = [(gate_t, gw, 0, KC * E)] + [(src, dst, a, min(STAGE, NX * D - a))
                                              for src, dst in ((exp_g, wg), (exp_u, wu), (exp_d, wd))
                                              for a in range(0, NX * D, STAGE)]
        staging = [h[:, :, :, :].rearrange("p a t f -> p (a t f)"), cwb[:, :, :, :].rearrange("p a e c -> p (a e c)")]

        @block.sync
        def _(sp):
            def load_z(c):
                for half in range(2):
                    row = c * C + (1 + B * half) * S
                    sp.dma_start(z[:, :, half * DH:(half + 1) * DH],
                                 z_rows[bass.ds(row, C), :].rearrange("(t p) f -> p t f", p=T)).then_inc(z_loaded, 16)

            def load_x(c):
                row = c * C
                sp.dma_start(x[:, :], x_rows[bass.ds(row, C), :].rearrange("(t p) f -> p t f", p=T)).then_inc(x_loaded, 16)

            def store(c):
                row = c * C
                sp.wait_ge(f_ready, c + 1)
                sp.dma_start(out_rows[bass.ds(row, C), :].rearrange("(t p) f -> p t f", p=T), fin[:, :, :]
                             ).then_inc(f_stored, 16)

            consts = ((w1[:, :, :], ff1), (w2[:, :, :], ff2), (b1[:, :], ff_bias1), (b2[:, :], ff_bias2),
                      (aff[:, :, :], affine), (gb[:, :], gate_bias), (low[:, :, :], lower),
                      (low4[:, :, :], lower[:, 0:NG, 0:NG]), (ident[:, :], identity))
            for dst, src in consts:
                sp.dma_start(dst, src).then_inc(const_loaded, 16)
            sp.sem_inc(f_stored, 16)
            for k, (src, _, a, n) in enumerate(pieces):
                if k >= 2:
                    sp.wait_ge(lo_made, k - 1)
                sp.dma_start(staging[k % 2][:, 0:n], src[:, a:a + n]).then_inc(raw_loaded[k % 2], 16)

            def period(P):
                if P.i == FIRST:
                    load_z(0)
                if P.next:
                    if P.i >= 0:
                        sp.wait_ge(cw_ready, P.num(1))
                    load_x(P.num(1))
                for e in range(0, E, CW):
                    if P.experts:
                        if P.i > 0 or e >= 2 * CW:
                            sp.wait_ge(weighted, P.at(lambda i: i * E) + e - CW)
                        sp.dma_start(cwb[:, e // CW % 2, :, :], cw_scratch[P.i % 2:P.i % 2 + 1, e:e + CW, :].broadcast_to([128, CW, C])
                                     ).then_inc(cw_loaded[e // CW % 2], 16)
                    if e == 2 * CW and P.next2 and P.i > FIRST:
                        sp.wait_ge(ring_read, P.ring("r", 1) + 1)
                        load_z(P.num(2))
                    if e == 4 * CW and P.prev:
                        store(P.num(-1))
                if P.next:
                    sp.wait_ge(ring_read, P.ring("cw") + 1)
                    sp.dma_start(cw_scratch[(P.i + 1) % 2, :, :], cwT[:, :]).then_inc(cw_stored, 16)
                    sp.wait_ge(cw_stored, 16 * P.num(2))
                    sp.sem_inc(s_passed, 1)

            run_periods(sp, period)
            store(CHUNKS - 1)
            sp.wait_ge(f_stored, 16 * (CHUNKS + 1))

        @block.tensor
        def _(pe):
            def exact(dst, lhs, rhs, start, stop):
                nc.tensor.matmul(dst, lhs[0], rhs[0], start=start, stop=False)
                nc.tensor.matmul(dst, lhs[0], rhs[1], start=False, stop=False)
                return nc.tensor.matmul(dst, lhs[1], rhs[0], start=False, stop=stop)

            def bank_of(P, job, j=0):
                idx = P.ring(job, j)
                if P.turn is not None or idx >= 2:
                    pe.wait_ge(ring_read, idx - 1)
                return p_ring[P.bank(job, j)]

            def turn_sums(P, job):
                for j in range(2):
                    bank = bank_of(P, job, j)
                    for t in range(2):
                        for f in range(KC):
                            tok = (2 * j + t) * T
                            last = nc.tensor.transpose(bank[:, t * D + f * 128:t * D + (f + 1) * 128],
                                                       turned[:, f * C + tok:f * C + tok + T], ident[:, :])
                    last.then_inc(ring_full, 1)

            def turn_tokens(P, job, src):
                for j in range(2):
                    bank = bank_of(P, job, j)
                    for t in range(TC):
                        last = nc.tensor.transpose(bank[:, t * T:(t + 1) * T], src[:, t, j * 128:(j + 1) * 128],
                                                   ident[:, :])
                    last.then_inc(ring_full, 1)

            def up(P, u):
                side = P.side(u)
                if P.units.index(u) >= LAG and u - LAG < NF or P.i == 0 and u < LAG:
                    pe.wait_ge(operand, P.unit(u) - 1)
                elif P.experts:
                    pe.wait_ge(product_made, P.at(lambda i: i * NX) + (u - NF if u >= NF else u) - 1)
                if u in (0, NF):
                    pe.wait_ge(ring_read, P.at(turns_before))
                if u < NF:
                    for k in range(KC):
                        last = nc.tensor.matmul(p_unit[side][:, 0, :], w1[:, k, u * 128:(u + 1) * 128], yT[:, k, :],
                                                start=(k == 0), stop=(k == KC - 1))
                else:
                    e = u - NF
                    for i, ws in enumerate((wg, wu)):
                        for k in range(KC):
                            cols = slice(e * D + k * 128, e * D + (k + 1) * 128)
                            last = exact(p_unit[side][:, i, :], [w_[:, cols] for w_ in ws],
                                         [p_[:, k, :] for p_ in hT[P.i % 2]], k == 0, k == KC - 1)
                last.then_inc(up_done, 1)

            def down(P, u):
                side = P.side(u)
                pe.wait_ge(operand, P.unit(u) + 1)
                if u == 0 and P.prev:
                    pe.wait_ge(sum_taken, P.num())
                if u == NF:
                    if P.next:
                        pe.wait_ge(ff_taken, P.num(2))
                    else:
                        pe.wait_ge(sum_taken, P.num())
                for f in range(KC):
                    if u < NF:
                        last = nc.tensor.matmul(p_acc[:, f, :], w2[:, u, f * 128:(f + 1) * 128], gated[side][:, :],
                                                start=(u == 0), stop=(u == NF - 1))
                    else:
                        cols = slice((u - NF) * D + f * 128, (u - NF) * D + (f + 1) * 128)
                        last = exact(p_acc[:, f, :], [w_[:, cols] for w_ in wd], (act_hi[side][:, :], act_lo[side][:, :]),
                                     u == NF, u == UNITS - 1)
                last.then_inc(down_done, 1)

            def steps(P, u):
                if P.prev and u == SLOT["f_turn"]:
                    pe.wait_ge(sum_taken, P.num())
                    turn_sums(P, "f")
                if P.next and u == SLOT["r_turn"]:
                    pe.wait_ge(ff_taken, P.num(2))
                    turn_sums(P, "r")
                if P.next and u == SLOT["h_turn"]:
                    pe.wait_ge(h_ready, P.num(2))
                    turn_tokens(P, "h", h[:, (P.i + 1) % 2, :, :])
                if P.next and u == SLOT["gate"]:
                    if P.i < 0:
                        pe.wait_ge(lo_made, 1)
                    pe.wait_ge(ring_read, P.ring("h", 1) + 1)
                    bank = bank_of(P, "gate")
                    for t in range(TC):
                        for k in range(KC):
                            last = exact(bank[:, t * E:(t + 1) * E], [p_[:, k, t * T:(t + 1) * T] for p_ in hT[(P.i + 1) % 2]],
                                         [w_[:, k * E:(k + 1) * E] for w_ in gw], k == 0, k == KC - 1)
                    last.then_inc(ring_full, 1)
                if P.next2 and u == SLOT["y_turn"]:
                    pe.wait_ge(y_ready, P.num(3))
                    turn_tokens(P, "y", z)
                if P.next and u == SLOT["cw_turn"]:
                    pe.wait_ge(cw_ready, P.num(2))
                    bank = bank_of(P, "cw")
                    for t in range(TC):
                        last = nc.tensor.transpose(bank[0:E, t * T:(t + 1) * T], cw[:, t, :], ident[:, :])
                    last.then_inc(ring_full, 1)

            def period(P):
                behind = []
                if P.carried:
                    last_period = Period(P.i - 1, P.turn)
                    behind = [(last_period, UNITS - 2), (last_period, UNITS - 1)]
                for u in range(UNITS):
                    if u in P.units:
                        if P.i == 0 and u == NF:
                            pe.wait_ge(lo_made, len(pieces))
                        up(P, u)
                        behind.append((P, u))
                    while len(behind) > (LAG if u in P.units else 0):
                        down(*behind.pop(0))
                    steps(P, u)
                if not P.carries:
                    for unit in behind:
                        down(*unit)

            pe.wait_ge(const_loaded, 9 * 16)
            run_periods(pe, period)
            pe.wait_ge(sum_taken, CHUNKS)
            turn_sums(Period(CHUNKS), "f")

        @block.scalar
        def _(act):
            act.wait_ge(const_loaded, 9 * 16)
            for k, (_, dst, a, n) in enumerate(pieces):
                act.wait_ge(raw_loaded[k % 2], 16 * (k // 2 + 1))
                nc.scalar.activation(dst[0][:, a:a + n], staging[k % 2][:, 0:n], ACT.Copy).then_inc(hi_made, 1)

            def period(P):
                for u in range(UNITS):
                    if u in P.units and u >= NF:
                        act.wait_ge(up_done, P.unit(u) + 1)
                        if P.next and u < NF + 2:
                            act.wait_ge(down_done, P.unit(u) - 1)
                        else:
                            act.wait_ge(operand, P.unit(u) - 1)
                        side = P.side(u)
                        nc.scalar.activation(gated[side][:, :], p_unit[side][:, 0, :], ACT.Silu).then_inc(silu_done, 1)
                    if P.next and u == NF + 1:
                        act.wait_ge(down_done, P.unit(NF - 1) + 1)
                        if P.prev:
                            act.wait_ge(ring_full, P.ring("f", 1) + 1)
                        for f in range(KC):
                            last = nc.scalar.activation(turned[:, f * C:(f + 1) * C], p_acc[:, f, :], ACT.Identity,
                                                        bias=b2[:, f:f + 1])
                        last.then_inc(ff_taken, 1)
                    if P.next and u == SLOT["gate_exp"]:
                        act.wait_ge(ring_read, P.ring("gate") + 1)
                        nc.scalar.activation(expo[:, :], logit[:, :], ACT.Exp, scale=-1.0).then_inc(gate_exped, 1)
                if P.experts:
                    act.wait_ge(down_done, P.unit(UNITS - 1) + 1)
                    if P.next:
                        act.wait_ge(cw_ready, P.num(2))
                    elif P.prev:
                        act.wait_ge(ring_full, P.ring("f", 1) + 1)
                    nc.scalar.activation(turned[:, :].rearrange("p (k c) -> p k c", k=KC), p_acc[:, :, :], ACT.Copy
                                         ).then_inc(sum_taken, 1)

            run_periods(act, period)

        @block.vector
        def _(dve):
            count = Count(2 * V_LINKS)

            def link(instruction):
                instruction.then_inc(v_step, 1)
                dve.wait_ge(v_step, count.next())

            def full(P, job, j=0):
                dve.wait_ge(ring_full, P.ring(job, j) + 1)
                return p_ring[P.bank(job, j)]

            def statistics(k, rows):
                n = len(rows)
                for i, row in enumerate(rows):
                    last = nc.vector.bn_stats(stats[k][:, i, :], row)
                link(last)
                dve.sem_inc(v_passed, 1)
                for i in range(n):
                    last = nc.vector.bn_aggr(mv[k][:, i, :], stats[k][:, i, :])
                link(last)
                nc.vector.tensor_scalar(var_eps[k][:, 0:n], mv[k][:, 0:n, 1], EPS, None, ALU.add
                                        ).then_inc(var_ready[k], 1)

            def normalise(k, rows, c):
                dve.wait_ge(scale_ready[k], c + 1)
                for i, row in enumerate(rows):
                    last = nc.vector.tensor_scalar(row, row, mv[k][:, i, 0:1], scale[k][:, i:i + 1],
                                                   ALU.subtract, ALU.mult)
                return last

            def normalise_affine(k, rows, factors, shifts, c):
                dve.wait_ge(scale_ready[k], c + 1)
                for i, row in enumerate(rows):
                    last = nc.vector.scalar_tensor_tensor(out=row, in0=row, scalar=mv[k][:, i, 0:1], in1=factors[i % len(factors)],
                                                          op0=ALU.subtract, op1=ALU.mult)
                link(last)
                for i, row in enumerate(rows):
                    last = nc.vector.scalar_tensor_tensor(out=row, in0=row, scalar=scale[k][:, i:i + 1], in1=shifts[i % len(shifts)],
                                                          op0=ALU.mult, op1=ALU.add)
                return last

            tiles = lambda buf: [buf[:, t, :] for t in range(TC)]
            halves = [z[:, t, f * DH:(f + 1) * DH] for t in range(TC) for f in range(2)]

            def take_unit(P, u):
                side = P.side(u)
                dve.wait_ge(up_done, P.unit(u) + 1)
                if u < NF:
                    if u >= 2:
                        dve.wait_ge(down_done, P.unit(u) - 1)
                    elif P.experts:
                        dve.wait_ge(operand, P.unit(u) - 1)
                    nc.vector.tensor_scalar(gated[side][:, :], p_unit[side][:, 0, :], b1[:, u:u + 1], 0.0,
                                            ALU.add, ALU.max).then_inc(operand, 1)
                    return
                if u - NF < E:
                    dve.wait_ge(weighted, P.at(lambda i: i * E) + u - NF + 1)
                else:
                    dve.wait_ge(silu_done, P.at(lambda i: i * NX) + u - NF + 1)
                nc.vector.tensor_tensor(gated[side][:, :], p_unit[side][:, 1, :], gated[side][:, :], ALU.mult
                                        ).then_inc(product_made, 1)
                dve.wait_ge(product_made, P.at(lambda i: i * NX) + u - NF + 1)
                dve.wait_ge(down_done, P.unit(u) - 1)
                link(nc.vector.tensor_copy(act_hi[side][:, :], gated[side][:, :]))
                nc.vector.tensor_tensor(act_lo[side][:, :], gated[side][:, :], act_hi[side][:, :].bitcast(F32),
                                        ALU.subtract).then_inc(operand, 1)

            def route_groups():
                link(nc.vector.tensor_scalar(expo[:, :], expo[:, :], 1.0, None, ALU.add))
                link(nc.vector.reciprocal(score[:, :], expo[:, :]))
                link(nc.vector.tensor_tensor(biased[:, :, :].rearrange("p (t g) e -> p t (g e)", t=TC),
                                             score[:, :].rearrange("p (t e) -> p t e", t=TC),
                                             gb[:, :].rearrange("p (o e) -> p o e", o=1).broadcast_to([T, TC, E]), ALU.add))
                for a, b_, at in ((slice(0, 2), slice(2, 4), slice(0, 2)), (slice(0, 3, 2), slice(1, 4, 2), slice(2, 4)),
                                  (slice(0, 1), slice(3, 4), slice(4, 5)), (slice(1, 2), slice(2, 3), slice(5, 6))):
                    last = nc.vector.tensor_tensor(pair_sum[:, :, at], biased[:, :, a], biased[:, :, b_], ALU.add)
                link(last)
                link(nc.vector.reduce_max(gscore[:, :, :].rearrange("p t g -> p (t g)"), pair_sum[:, :, :], AX.X))
                other = gscore[:, :, :].rearrange("p t (o g) -> p t o g", o=1).broadcast_to([T, TC, NG, NG])
                own = gscore[:, :, :].rearrange("p t (g o) -> p t g o", o=1).broadcast_to([T, TC, NG, NG])
                nc.vector.tensor_tensor(gcmp[0][:, :, :, :], other, own, ALU.is_gt)
                link(nc.vector.tensor_tensor(gcmp[1][:, :, :, :], other, own, ALU.is_equal))
                link(nc.vector.tensor_tensor(gcmp[1][:, :, :, :], gcmp[1][:, :, :, :],
                                             low4[:, :, :].rearrange("p (o i) j -> p o i j", o=1).broadcast_to([T, TC, NG, NG]), ALU.mult))
                link(nc.vector.tensor_tensor(gcmp[0][:, :, :, :], gcmp[0][:, :, :, :], gcmp[1][:, :, :, :], ALU.add))
                link(nc.vector.reduce_sum(grank[:, :], gcmp[0][:, :, :, :].rearrange("p t i j -> p (t i) j"), AX.X))
                link(nc.vector.tensor_scalar(grank[:, :], grank[:, :], float(TOPG), None, ALU.is_lt))
                link(nc.vector.tensor_scalar(gpen[:, :], grank[:, :], -1.0, BIG, ALU.add, ALU.mult))
                spread = lambda v: v[:, :].rearrange("p (g o) -> p g o", o=1).broadcast_to([T, TC * NG, EG])
                link(nc.vector.tensor_tensor(masked[:, :, :], biased[:, :, :], spread(grank), ALU.mult))
                link(nc.vector.tensor_tensor(masked[:, :, :], masked[:, :, :], spread(gpen), ALU.add))

            def route_experts():
                m = masked[:, :, :].rearrange("p (t g) e -> p t (g e)", t=TC)
                other = m.rearrange("p t (o e) -> p t o e", o=1).broadcast_to([T, TC, E, E])
                own = m.rearrange("p t (e o) -> p t e o", o=1).broadcast_to([T, TC, E, E])
                nc.vector.tensor_tensor(ecmp[0], other, own, ALU.is_gt)
                link(nc.vector.tensor_tensor(ecmp[1], other, own, ALU.is_equal))
                link(nc.vector.tensor_tensor(ecmp[1], ecmp[1],
                                             low[:, :, :].rearrange("p (o i) j -> p o i j", o=1).broadcast_to([T, TC, E, E]), ALU.mult))

            def route_weights():
                link(nc.vector.tensor_tensor(ecmp[0], ecmp[0], ecmp[1], ALU.add))
                link(nc.vector.reduce_sum(erank[:, :], ecmp[0].rearrange("p t i j -> p (t i) j"), AX.X))
                link(nc.vector.tensor_scalar(erank[:, :], erank[:, :], float(TOPK), None, ALU.is_lt))
                link(nc.vector.tensor_tensor(wsel[:, :, :].rearrange("p t e -> p (t e)"), erank[:, :], score[:, :], ALU.mult))
                link(nc.vector.reduce_sum(wsum[:, :], wsel[:, :, :], AX.X))
                link(nc.vector.tensor_scalar(wsum[:, :], wsum[:, :], 1e-20, None, ALU.add))
                link(nc.vector.reciprocal(wsum[:, :], wsum[:, :]))
                link(nc.vector.tensor_tensor(wsel[:, :, :], wsel[:, :, :],
                                             wsum[:, :].rearrange("p (t o) -> p t o", o=1).broadcast_to([T, TC, E]), ALU.mult))
                nc.vector.tensor_scalar(cw[:, :, :], wsel[:, :, :], ROUTED_SCALE, None, ALU.mult).then_inc(cw_ready, 1)

            def steps(P, u):
                hp = (P.i + 1) % 2
                two = lambda buf, j: buf[:, 2 * j:2 * j + 2, :]
                pairs_of = lambda bank: bank[:, :].rearrange("p (t f) -> p t f", t=2)
                if P.prev and u == SLOT["f_add"]:
                    dve.wait_ge(f_stored, 16 * P.num())
                    add_final(P)
                if P.prev and u == SLOT["f_norm"]:
                    normalise("f", tiles(fin), P.num(-1)).then_inc(f_ready, 1)
                if P.next and u == SLOT["r_add"]:
                    for j in range(2):
                        bank = full(P, "r", j)
                        last = nc.vector.tensor_tensor(two(h[:, hp, :, :], j), pairs_of(bank), two(z, j), ALU.add)
                        last.then_inc(ring_read, 1)
                    dve.wait_ge(ring_read, P.ring("r", 1) + 1)
                    statistics("r", tiles(h[:, hp, :, :]))
                if P.next and u == SLOT["r_norm"]:
                    link(normalise_affine("r", tiles(h[:, hp, :, :]), [aff[:, 2, :]], [aff[:, 3, :]], P.num(1)))
                if P.next and u == SLOT["s_add"]:
                    dve.wait_ge(x_loaded, 16 * P.num(2))
                    link(nc.vector.tensor_tensor(h[:, hp, :, :].rearrange("p t f -> p (t f)"), h[:, hp, :, :].rearrange("p t f -> p (t f)"),
                                                 x[:, :], ALU.add))
                    statistics("s", tiles(h[:, hp, :, :]))
                if P.next and u == SLOT["s_norm"]:
                    normalise("s", tiles(h[:, hp, :, :]), P.num(1)).then_inc(h_ready, 1)
                if P.next and u == SLOT["h_take"]:
                    for j in range(2):
                        bank = full(P, "h", j)
                        link(nc.vector.tensor_copy(hT[hp][0][:, j, :], bank[:, :]))
                        nc.vector.tensor_tensor(hT[hp][1][:, j, :], bank[:, :], hT[hp][0][:, j, :].bitcast(F32),
                                                ALU.subtract).then_inc(ring_read, 1)
                if P.next and u == SLOT["gate_take"]:
                    nc.vector.tensor_copy(logit[:, :], full(P, "gate")[:, 0:TC * E]).then_inc(ring_read, 1)
                if P.next2 and u == SLOT["z_stats"]:
                    dve.wait_ge(z_loaded, 32 * P.num(3))
                    statistics("z", halves)
                if P.next2 and u == SLOT["z_norm"]:
                    of_half = lambda j: [aff[:, j, f * DH:(f + 1) * DH] for f in range(2)]
                    normalise_affine("z", halves, of_half(0), of_half(1), P.num(2)).then_inc(y_ready, 1)
                if P.next2 and u == SLOT["y_take"]:
                    for j in range(2):
                        nc.vector.tensor_copy(yT[:, j, :], full(P, "y", j)[:, :]).then_inc(ring_read, 1)
                if P.next and u == SLOT["route_groups"]:
                    dve.wait_ge(gate_exped, P.num(2))
                    route_groups()
                if P.next and u == SLOT["route_experts"]:
                    route_experts()
                if P.next and u == SLOT["route_weights"]:
                    route_weights()
                if P.next and u == SLOT["cw_take"]:
                    if P.i >= 0:
                        dve.wait_ge(cw_stored, 16 * P.num(1))
                    nc.vector.tensor_copy(cwT[:, :], full(P, "cw")[0:E, :]).then_inc(ring_read, 1)

            def add_final(P):
                for j in range(2):
                    bank = full(P, "f", j)
                    last = nc.vector.scalar_tensor_tensor(
                        out=fin[:, 2 * j:2 * j + 2, :].rearrange("p t f -> p (t f)"),
                        in0=h[:, (P.i - 1) % 2, 2 * j:2 * j + 2, :].rearrange("p t f -> p (t f)"), scalar=2.0,
                        in1=bank[:, :], op0=ALU.mult, op1=ALU.add)
                    last.then_inc(ring_read, 1)
                dve.wait_ge(ring_read, P.ring("f", 1) + 1)
                statistics("f", tiles(fin))

            def period(P):
                for u in range(UNITS):
                    if u in P.units:
                        take_unit(P, u)
                    steps(P, u)

            dve.wait_ge(const_loaded, 9 * 16)
            for k, (_, dst, a, n) in enumerate(pieces):
                dve.wait_ge(hi_made, k + 1)
                nc.vector.tensor_tensor(dst[1][:, a:a + n], staging[k % 2][:, 0:n], dst[0][:, a:a + n].bitcast(F32),
                                        ALU.subtract).then_inc(lo_made, 1)
            run_periods(dve, period, count)
            last_period = Period(CHUNKS)
            dve.wait_ge(f_stored, 16 * CHUNKS)
            add_final(last_period)
            normalise("f", tiles(fin), CHUNKS - 1).then_inc(f_ready, 1)

        @block.gpsimd
        def _(pool):
            def inverse_root(k, n, c):
                pool.wait_ge(var_ready[k], c + 1)
                nc.gpsimd.tensor_tensor(scale[k][:, 0:n], var_eps[k][:, 0:n], power[:, 0:n], ALU.pow
                                        ).then_inc(scale_ready[k], 1)

            nc.gpsimd.memset(power[:, :], -0.5).then_inc(power_set, 1)
            pool.wait_ge(power_set, 1)
            pool.wait_ge(const_loaded, 9 * 16)

            def steps(P, u):
                if P.prev and u == SLOT["f_scale"]:
                    inverse_root("f", TC, P.num(-1))
                if P.next and u == SLOT["r_scale"]:
                    inverse_root("r", TC, P.num(1))
                if P.next and u == SLOT["s_scale"]:
                    inverse_root("s", TC, P.num(1))
                if P.next2 and u == SLOT["z_scale"]:
                    inverse_root("z", 2 * TC, P.num(2))

            def period(P):
                for u in range(UNITS):
                    if u in P.units and NF <= u < NF + E:
                        e, side = u - NF, P.side(u)
                        pool.wait_ge(silu_done, P.at(lambda i: i * NX) + e + 1)
                        pool.wait_ge(cw_loaded[e // CW % 2], 16 * (P.at(lambda i: i * E // (2 * CW)) + e // (2 * CW) + 1))
                        nc.gpsimd.tensor_tensor(gated[side][:, :], gated[side][:, :], cwb[:, e // CW % 2, e % CW, :],
                                                ALU.mult).then_inc(weighted, 1)
                    steps(P, u)

            run_periods(pool, period)
            inverse_root("f", TC, CHUNKS - 1)


def build(nc, a, out):
    xT_pairs = nc.dram_tensor("xT_pairs", [PAIRS + 1, DH, S], F32, kind="Internal").ap()
    xN_pairs = nc.dram_tensor("xN_pairs", [PAIRS + 1, S, DH], F32, kind="Internal").ap()
    z_pairs = nc.dram_tensor("z_pairs", [PAIRS + 1, S, DH], F32, kind="Internal").ap()
    attention(nc, a["x_tok"], a["x_feat"], a["holt_in"], a["holt_state"], a["holt_out"], a["holt_carry"], a["x0_rows"],
              a["w_pairs"], a["bias_qk"], a["bias_v"], a["bias_o"], a["identity"], xT_pairs, xN_pairs, z_pairs)
    experts(nc, a["x_tok"], z_pairs, a["ff1"], a["ff2"], a["gate_t"], a["exp_g"], a["exp_u"], a["exp_d"],
            a["ff_bias1"], a["ff_bias2"], a["affine"], a["gate_bias"], a["lower"], a["identity"], out)


def holt_constants():
    import numpy as np

    step = np.array([[1 - ALPHA, 1 - ALPHA], [-ALPHA * BETA, 1 - ALPHA * BETA]])
    gain = np.array([ALPHA, ALPHA * BETA])
    powers = [np.eye(2)]
    for _ in range(S):
        powers.append(powers[-1] @ step)
    levels = np.zeros((T, T))
    for t in range(T):
        for u in range(t + 1):
            levels[u, t] = (powers[t - u] @ gain)[0]
    state_level = np.zeros((2 * NT, NT, T))
    x_state = np.zeros((T, NT, 2 * NT))
    state_state = np.zeros((2, 2 * NT))
    for c in range(NT):
        state_level[2 * c:2 * c + 2, c] = np.stack([powers[t + 1][0] for t in range(T)], 1)
        state_state[:, 2 * c:2 * c + 2] = powers[c * T].T
        for before in range(c):
            x_state[:, before, 2 * c:2 * c + 2] = [powers[(c - before) * T - 1 - u] @ gain for u in range(T)]
    return [a.astype(np.float32) for a in (levels, state_level, x_state, state_state)]


def kernel(**inputs):
    import numpy as np
    import concourse.bacc as bacc
    from concourse.bass_utils import run_bass_kernel_spmd

    f = {k.removeprefix("L0_"): np.asarray(v) for k, v in inputs.items()}
    att = lambda name: f["attn_" + name]
    x = att("x")
    every = lambda v: np.broadcast_to(v, (T,) + v.shape)
    branch = [1] * B + [2] * B + [1]
    half = lambda w: w.reshape(KC, 128, -1).transpose(1, 0, 2)

    def expert_cols(routed, shared):
        w = np.concatenate([routed, shared.reshape(2, 128, D)]).reshape(NX, 128, KC, 128)
        return w.transpose(3, 0, 2, 1).reshape(128, NX * D)

    down = np.concatenate([f["ffn_Wd"], f["ffn_Ws_d"].reshape(D, 2, 128).transpose(1, 0, 2)])
    x0 = np.zeros((2, B, DH), np.float32)
    x0[0] = x[:, 0, :DH]
    levels, state_level, x_state, state_state = holt_constants()
    arrays = {
        "x_tok": x,
        "x_feat": x[:, :, :DH].transpose(0, 2, 1),
        "holt_in": levels, "holt_state": state_level, "holt_out": x_state, "holt_carry": state_state,
        "x0_rows": x0.reshape(2, B * DH),
        "w_pairs": np.stack([np.concatenate([att(f"w{c}{a}").T for c in "qkvo"], 1) for a in branch]),
        "bias_qk": np.stack([np.stack([att(f"bq{a}"), att(f"bk{a}")], 1) for a in branch]),
        "bias_v": np.stack([every(att(f"bv{a}")) for a in branch]),
        "bias_o": np.stack([every(att(f"bo{a}")) for a in branch]),
        "identity": np.eye(128, dtype=np.float32),
        "ff1": half(att("w_ff1").T),
        "ff2": att("w_ff2").T.reshape(NF, 128, D).transpose(1, 0, 2),
        "gate_t": half(f["ffn_gate_w"].T).reshape(128, KC * E),
        "exp_g": expert_cols(f["ffn_Wg"], f["ffn_Ws_g"]),
        "exp_u": expert_cols(f["ffn_Wu"], f["ffn_Ws_u"]),
        "exp_d": down.transpose(2, 0, 1).reshape(128, NX * D),
        "ff_bias1": att("b_ff1").reshape(NF, 128).T,
        "ff_bias2": att("b_ff2").reshape(KC, 128).T,
        "affine": every(np.stack([np.concatenate([att("g1"), att("g2")]), np.concatenate([att("be1"), att("be2")]),
                                  att("g_ff"), att("be_ff")])),
        "gate_bias": every(f["ffn_gate_bias"]),
        "lower": every(np.tril(np.ones((E, E), np.float32), -1)),
    }
    nc = bacc.Bacc("TRN2", target_bir_lowering=False, num_devices=1)
    arrays = {k: np.ascontiguousarray(v) for k, v in arrays.items()}
    ap = {k: nc.dram_tensor("in_" + k, v.shape, mybir.dt.from_np(v.dtype), kind="ExternalInput").ap()
          for k, v in arrays.items()}
    out = nc.dram_tensor("out", (B, S, D), F32, kind="ExternalOutput").ap()
    build(nc, ap, out)
    r = run_bass_kernel_spmd(nc, [{"in_" + k: v for k, v in arrays.items()}], core_ids=[0])
    return r.results[0]["out"]
```

```python
import concourse.bass as bass
from concourse import mybir
from contextlib import ExitStack

F32 = mybir.dt.float32
BF16 = mybir.dt.bfloat16
ALU = mybir.AluOpType
ACT = mybir.ActivationFunctionType
AX = mybir.AxisListType

B, S, D = 4, 2048, 256
DH = D // 2
H, DK = 8, 16
T = 128
C = 512
NCH = S // C
NT = S // T
TC = C // T
G = 4
PAIRS = 2 * B
ALPHA, BETA, EPS = 0.1, 0.1, 1e-5


PERIODS = 2 * NCH
STEPS = NT
RING = 3


def extras(p, k):
    out = []
    if k == 1:
        out.append(("max_rows",))
    if k == 2:
        out.append(("o_tok",))
    if (p - 1) % PERIODS >= NCH:
        if k == 4:
            out.append(("o_feat",))
        if k == 6:
            out.append(("project",))
    if p in (2, 3):
        if k in (3, 5, 8, 10):
            i = (p - 2) * 4 + (3, 5, 8, 10).index(k)
            out.append(("qk", i % 2, i // 2))
        if k in (12, 13, 14) and (p, k) != (3, 14):
            i = (p - 2) * 3 + k - 12
            out.append(("v", (0, 4, 8, 12, 14)[i], (4, 4, 4, 2, 2)[i]))
    return out


def ring_jobs():
    at, n = {}, 0
    for p in range(PERIODS):
        for k in range(STEPS):
            for h in range(G):
                at[p, k, "max", h] = n
                n += 1
            for e in extras(p, k):
                at[(p, k) + e] = n
                n += 1
    return at, n


ORDER = [("score", 0), ("max", 0), ("score", 1), ("score", 2), ("max", 1), ("score", 3), ("max", 2), "weigh", ("max", 3)]
JOB, JOBS = ring_jobs()
assert JOBS % RING == 0
RUN_IN = ([("qk", w, c) for w in (1, 0) for c in range(NCH)] + [("v", t, 4) for t in range(0, NT, 4)]
          + [("max", 0, k, h) for k in range(STEPS) for h in range(G)] + [("max_rows",)]
          + [("max", 1, k, h) for k in range(STEPS) for h in range(G)])
R0 = len(RUN_IN)
Q_PART = (0, 0, 1, 0, 1, 2)
K_PART = (0, 1, 0, 2, 1, 0)
STACK = 2 * len(Q_PART) * G
COPIES = 4
ROWS = DK * len(Q_PART)


def attention(nc, x_tok, x_feat, holt_in, holt_state, holt_out, holt_carry, x0_rows,
              w_pairs, bias_qk, bias_v, bias_o, identity, xT_pairs, xN_pairs, z_pairs):
    with ExitStack() as ctx:
        sb = lambda name, shape, dt=F32: ctx.enter_context(nc.sbuf_tensor(name, shape, dt))
        sem = lambda name: ctx.enter_context(nc.semaphore(name))
        ks = [sb(f"k_rows{g}", [128, G, S], BF16) for g in range(2)]
        qs = [sb("q_rows0", [128, G, S], BF16)]
        qk_part = [[sb(f"{x}_part{i}", [128, S], BF16) for i in range(3)] for x in "qk"]
        va = sb("v_ones", [T, NT, H, 2 * DK])
        vs = sb("v_stage", [T, NT, DH])
        xT = sb("x_feat", [DH, S])
        w = sb("w_qkv", [DH, 3 * DH])
        wo = sb("w_o", [DH, DH])
        bqk = sb("b_qk", [DH, 2])
        bv = sb("b_v", [T, DH])
        bo = sb("b_o", [T, DH])
        ident = sb("ident", [128, 128])
        qk_f = [sb(f"qk_f{i}", [DH, C]) for i in range(2)]
        rest = sb("qk_rest", [DH, C])
        mpart = [sb(f"max_part{i}", [T, G * TC, NCH]) for i in range(2)]
        mneg = sb("max_neg", [T, G * TC])
        mrow = sb("max_row", [G * TC, 2, T], BF16)
        max_scratch = nc.dram_tensor("max_scratch", [2, G * TC, T], BF16, kind="Internal").ap()
        o_raw = sb("o_raw", [T, C])
        o_tok = sb("o_tok", [T, NT, DH])
        with ExitStack() as early:
            hb = lambda name, shape: early.enter_context(nc.sbuf_tensor(name, shape, F32))
            hx = hb("holt_x", [T, NT, B, DH])
            lin = hb("holt_lin", [T, T])
            lstate = hb("holt_lstate", [2 * NT, NT, T])
            lout = hb("holt_lout", [T, NT, 2 * NT])
            carry = hb("holt_carry", [2, 2 * NT])
            first = hb("holt_first", [2, B * DH])
            states = hb("holt_states", [2 * NT, B * DH])
            level = hb("holt_level", [T, 2, B * DH])
            level_T = hb("holt_level_T", [DH, 2, B, C])
        qs.append(sb("q_rows1", [128, G, S], BF16))
        prob = [sb(f"prob{i}", [T, G, C]) for i in range(2)]
        o_rec = sb("o_rec", [T, TC, G])
        o_feat = sb("o_feat", [DH, C])
        res = [sb(f"res{i}", [T, TC, DH]) for i in range(2)]
        res_b = sb("res_b", [T, TC, DH])
        z = [sb(f"z{i}", [T, TC, DH]) for i in range(2)]

        p_exp = [ctx.enter_context(nc.psum_tensor(f"p_exp{i}", [T, 2, C], F32)) for i in range(2)]
        p_ring = [ctx.enter_context(nc.psum_tensor(f"p_ring{i}", [128, C], F32)) for i in range(RING)]
        p_av = ctx.enter_context(nc.psum_tensor("p_av", [128, C], F32))
        p_level, p_turned, p_states = p_exp[0], p_exp[1], p_av[0:2 * NT, :]

        once = sem("once_loaded")
        holt_loaded, copied = sem("holt_loaded"), sem("copied")
        states_summed, states_set = sem("states_summed"), sem("states_set")
        level_made, level_out = sem("level_made"), sem("level_out")
        turned_made, turned_out = sem("turned_made"), sem("turned_out")
        level_stored = [sem(f"level_stored{i}") for i in range(2)]
        turned_stored = [sem(f"turned_stored{i}") for i in range(2)]
        qkv_loaded, o_loaded = sem("qkv_loaded"), sem("o_loaded")
        ones_set = sem("ones_set")
        ring_full, ring_read = sem("ring_full"), sem("ring_read")
        parts_ready, stacked = sem("parts_ready"), sem("stacked")
        split_step = sem("split_step")
        pool_passed, sp_passed = sem("pool_passed"), sem("sp_passed")
        v_copied = sem("v_copied")
        max_neg, max_high = sem("max_neg"), sem("max_high")
        rows_out, rows_stored = sem("rows_out"), sem("rows_stored")
        scored, exped, summed = sem("scored"), sem("exped"), sem("summed")
        o_raw_ready, o_rec_ready = sem("o_raw_ready"), sem("o_rec_ready")
        res_loaded, res_ready = sem("res_loaded"), sem("res_ready")
        z_stored = [sem(f"z_stored{i}") for i in range(2)]
        block = ctx.enter_context(nc.Block())

        ring_of = lambda n, job: n * JOBS + R0 + job
        step_of = lambda n, p, k: n * PERIODS * STEPS + p * STEPS + k
        finishes = lambda p: (p - 1) % PERIODS >= NCH
        FIN = [p for p in range(PERIODS) if finishes(p)]

        def stack_rows(queue, x, g, blocks=range(len(Q_PART))):
            rows, parts = ((qs[g], Q_PART), (ks[g], K_PART))[x]
            for j in blocks:
                i = parts[j]
                for h in range(G):
                    src = (g * G + h) * DK
                    queue.dma_start(rows[j * DK:(j + 1) * DK, h, :], qk_part[x][i][src:src + DK, :]
                                    ).then_inc(stacked, 16)

        @block.sync
        def _(sp):
            def load_qkv(n, x=None):
                sp.dma_start(w[:, :], w_pairs[n, :, 0:3 * DH]).then_inc(qkv_loaded, 16)
                sp.dma_start(bqk[:, :], bias_qk[n, :, :]).then_inc(qkv_loaded, 16)
                sp.dma_start(bv[:, :], bias_v[n, :, :]).then_inc(qkv_loaded, 16)
                sp.dma_start(xT[:, :], xT_pairs[n, :, :] if x is None else x).then_inc(qkv_loaded, 16)

            def load_o(n):
                sp.dma_start(wo[:, :], w_pairs[n, :, 3 * DH:4 * DH]).then_inc(o_loaded, 16)
                sp.dma_start(bo[:, :], bias_o[n, :, :]).then_inc(o_loaded, 16)

            def stack(g):
                for x in range(2):
                    stack_rows(sp, x, g)

            def store_rows(n, u, job):
                sp.wait_ge(ring_read, ring_of(n, job) + 1)
                g, c = u // NCH % 2, u % NCH
                sp.dma_start(max_scratch.rearrange("i r s -> r i s"), mrow[:, :, :]).then_inc(rows_out, 16)
                sp.wait_ge(rows_out, 16 * (n * PERIODS + u + 1))
                sp.dma_start(qs[g][ROWS:ROWS + 2, :, c * C:(c + 1) * C],
                             max_scratch.rearrange("i (h t) s -> i h (t s)", h=G)).then_inc(rows_stored, 16)

            def load_res(n, i, pair, c, f):
                sp.wait_ge(res_ready, n * len(FIN) + f + 1)
                sp.dma_start(res[i][:, :, :], xN_pairs[pair, c * C:(c + 1) * C, :].rearrange("(t p) f -> p t f", p=T)
                             ).then_inc(res_loaded, 16)

            def store_z(n, i, pair, c, job):
                sp.wait_ge(ring_read, ring_of(n, job) + 1)
                sp.dma_start(z_pairs[pair, c * C:(c + 1) * C, :].rearrange("(t p) f -> p t f", p=T),
                             z[i][:, :, :]).then_inc(z_stored[i], 16)

            for i in range(2):
                sp.sem_inc(z_stored[i], 16)
            sp.sem_inc(res_ready, 2)
            sp.dma_start(ident[:, :], identity).then_inc(once, 16)
            load_qkv(0, x_feat[0, :, :])
            load_o(0)
            for dst, src in [(lout[:, :, :], holt_out), (carry[:, :], holt_carry), (first[:, :], x0_rows),
                             (lin[:, :], holt_in), (lstate[:, :, :], holt_state)] + [
                                 (hx[:, :, b, :], x_tok[b, :, 0:DH].rearrange("(c t) f -> t c f", t=T)) for b in range(B)]:
                sp.dma_start(dst, src).then_inc(holt_loaded, 16)
            sp.wait_ge(parts_ready, 2 * NCH)
            stack_rows(sp, 0, 0, range(0, len(Q_PART) // 2))
            store_rows(0, 0, RUN_IN.index(("max_rows",)) - R0)
            sp.wait_ge(copied, 16 * COPIES)
            for i in range(2):
                sp.wait_ge(level_stored[i], 16 * NT // 2)
                sp.wait_ge(turned_stored[i], 16 * NCH // 2)

            def period(n, p):
                if finishes(p):
                    f = FIN.index(p)
                    load_res(n, f % 2, n if p == 0 else n + 1, (p - 1) % NCH, f)
                if p == 0:
                    sp.wait_ge(ring_full, ring_of(n, 0))
                    stack(1)
                if p == 1:
                    sp.wait_ge(ring_read, ring_of(n, JOB[1, 0, "max", 0]))
                    load_qkv(n + 1)
                    load_o(n)
                store_rows(n, p + 1, JOB[p, 1, "max_rows"])
                if p == NCH:
                    sp.wait_ge(scored, 2 * step_of(n, NCH, 0))
                    sp.sem_inc(sp_passed, 1)
                    sp.wait_ge(parts_ready, 2 * NCH * n + 4 * NCH)
                    stack(0)
                if finishes(p):
                    store_z(n, f % 2, n if p == 0 else n + 1, (p - 1) % NCH, JOB[p, 6, "project"])

            with sp.Fori(0, PAIRS) as n:
                for p in range(PERIODS):
                    period(n, p)
            load_res(PAIRS, 0, PAIRS, NCH - 1, 0)
            store_z(PAIRS, 0, PAIRS, NCH - 1, 2)
            sp.wait_ge(z_stored[0], 16 * (2 * PAIRS + 2))
            sp.wait_ge(z_stored[1], 16 * (2 * PAIRS + 1))
            sp.wait_ge(stacked, 16 * STACK * (2 * PAIRS + 1))
            sp.wait_ge(rows_stored, 16 * (PERIODS * PAIRS + 1))
            sp.wait_ge(qkv_loaded, 64 * (PAIRS + 1))

        @block.tensor
        def _(pe):
            def ring_bank(n, job):
                idx = ring_of(n, job)
                if not isinstance(n, int) or idx >= RING:
                    pe.wait_ge(ring_read, idx - RING + 1)
                return p_ring[(R0 + job) % RING]

            def max_scores(n, job, g, c, k, h):
                bank = ring_bank(n, job)
                q0, k0 = c * C + (k // NCH) * T, (k % NCH) * C
                nc.tensor.matmul(bank[:, :], qs[g][0:ROWS, h, q0:q0 + T], ks[g][0:ROWS, h, k0:k0 + C],
                                 start=True, stop=True).then_inc(ring_full, 1)

            def max_rows(n, job, done):
                bank = ring_bank(n, job)
                pe.wait_ge(max_neg, done)
                nc.tensor.transpose(bank[0:G * TC, 0:T], mneg[:, :], ident[:, :]).then_inc(ring_full, 1)

            def project_qk(n, job, which, c):
                bank = ring_bank(n, job)
                nc.tensor.matmul(bank[:, :], w[:, which * DH:(which + 1) * DH], xT[:, c * C:(c + 1) * C],
                                 start=True, stop=True).then_inc(ring_full, 1)

            def project_v(n, job, t0, count):
                bank = ring_bank(n, job)
                for i in range(count):
                    last = nc.tensor.matmul(bank[:, i * DH:(i + 1) * DH], xT[:, (t0 + i) * T:(t0 + i + 1) * T],
                                            w[:, 2 * DH:3 * DH], start=True, stop=True)
                last.then_inc(ring_full, 1)

            def score(n, p, k, h):
                g, c, pair = p // NCH, p % NCH, h // 2
                if h % 2 == 0 and (p or k):
                    pe.wait_ge(exped, 2 * step_of(n, p, k) + pair - 1)
                product = nc.tensor.matmul(p_exp[pair][:, h % 2, :], ks[g][0:ROWS + 2, h, k * T:(k + 1) * T],
                                           qs[g][0:ROWS + 2, h, c * C:(c + 1) * C], start=True, stop=True)
                if h % 2:
                    product.then_inc(scored, 1)

            def weigh(n, p, k):
                pe.wait_ge(exped, 2 * step_of(n, p, k) + 2)
                if k == 0:
                    pe.wait_ge(o_raw_ready, n * PERIODS + p + 1)
                    if p % NCH == 0:
                        pe.wait_ge(v_copied, 2 * n + p // NCH + 1)
                for h in range(G):
                    last = nc.tensor.matmul(p_av[32 * h:32 * h + 2 * DK, :], va[:, k, p // NCH * G + h, :],
                                            prob[k % 2][:, h, :], start=(k == 0), stop=(k == STEPS - 1))
                last.then_inc(summed, 1)

            def outputs_to_tokens(n, job, done):
                bank = ring_bank(n, job)
                pe.wait_ge(o_raw_ready, done)
                for t in range(TC):
                    last = nc.tensor.transpose(bank[:, t * T:(t + 1) * T], o_raw[:, t * T:(t + 1) * T], ident[:, :])
                last.then_inc(ring_full, 1)

            def outputs_to_features(n, job, after, c):
                bank = ring_bank(n, job)
                pe.wait_ge(ring_read, ring_of(n, after) + 1)
                for t in range(TC):
                    last = nc.tensor.transpose(bank[:, t * T:(t + 1) * T], o_tok[:, c * TC + t, :], ident[:, :])
                last.then_inc(ring_full, 1)

            def project_out(n, job, after):
                bank = ring_bank(n, job)
                pe.wait_ge(ring_read, ring_of(n, after) + 1)
                for t in range(TC):
                    last = nc.tensor.matmul(bank[:, t * DH:(t + 1) * DH], o_feat[:, t * T:(t + 1) * T], wo[:, :],
                                            start=True, stop=True)
                last.then_inc(ring_full, 1)

            def sum_states():
                pe.wait_ge(holt_loaded, 9 * 16)
                nc.tensor.matmul(p_states, carry[:, :], first[:, :], start=True, stop=False)
                for c in range(NT - 1):
                    last = nc.tensor.matmul(p_states, lout[:, c, :], hx[:, c, :, :].rearrange("t b f -> t (b f)"),
                                            start=False, stop=(c == NT - 2))
                last.then_inc(states_summed, 1)

            def levels(c):
                pe.wait_ge(states_set, 1)
                if c >= 2:
                    pe.wait_ge(level_out, c - 1)
                nc.tensor.matmul(p_level[:, c % 2, :], lin[:, :], hx[:, c, :, :].rearrange("t b f -> t (b f)"),
                                 start=True, stop=False)
                nc.tensor.matmul(p_level[:, c % 2, :], lstate[:, c, :], states[:, :], start=False, stop=True
                                 ).then_inc(level_made, 1)

            def turn_levels(c):
                pe.wait_ge(level_out, c + 1)
                if c >= 2:
                    pe.wait_ge(turned_out, c - 1)
                for b in range(B):
                    last = nc.tensor.transpose(p_turned[:, c % 2, b * T:(b + 1) * T],
                                               level[:, c % 2, b * DH:(b + 1) * DH], ident[:, :])
                last.then_inc(turned_made, 1)

            pe.wait_ge(once, 16)
            pe.wait_ge(o_loaded, 32)
            pe.wait_ge(qkv_loaded, 64)
            for i, job in enumerate(RUN_IN):
                if job == ("max", 0, 0, 0):
                    sum_states()
                if job[0] == "qk":
                    project_qk(0, i - R0, job[1], job[2])
                elif job[0] == "v":
                    project_v(0, i - R0, job[1], job[2])
                elif job[0] == "max_rows":
                    max_rows(0, i - R0, 1)
                else:
                    if job == ("max", 0, 0, 0):
                        pe.wait_ge(stacked, 16 * STACK)
                    max_scores(0, i - R0, 0, job[1], job[2], job[3])
                    at = (job[1] * STEPS + job[2]) * G + job[3]
                    if at % 7 == 1 and at // 7 < NT:
                        levels(at // 7)
                    if at % 7 == 4 and at // 7 < NT:
                        turn_levels(at // 7)
            pe.wait_ge(level_out, NT)
            pe.wait_ge(turned_out, NT)

            def extra(n, p, k, e):
                job = JOB[(p, k) + e]
                if e[0] == "max_rows":
                    max_rows(n, job, n * PERIODS + p + 2)
                elif e[0] == "o_tok":
                    outputs_to_tokens(n, job, n * PERIODS + p + 1)
                elif e[0] == "o_feat":
                    outputs_to_features(n, job, JOB[p, 2, "o_tok"], (p - 1) % NCH)
                elif e[0] == "project":
                    if p == 5:
                        pe.wait_ge(o_loaded, 32 * n + 64)
                    project_out(n, job, JOB[p, 4, "o_feat"])
                elif e[0] == "qk":
                    if e[1:] == (0, 0):
                        pe.wait_ge(qkv_loaded, 64 * n + 128)
                    project_qk(n, job, e[1], e[2])
                else:
                    project_v(n, job, e[1], e[2])

            with pe.Fori(0, PAIRS) as n:
                for p in range(PERIODS):
                    u = p + 2
                    for k in range(STEPS):
                        if k == 0:
                            pe.wait_ge(rows_stored, 16 * (n * PERIODS + p + 1))
                            if u % NCH == 0:
                                pe.wait_ge(stacked, 16 * STACK * (2 * n + u // NCH + 1))
                        for part in ORDER:
                            if part == "weigh":
                                if k:
                                    weigh(n, p, k - 1)
                                elif p:
                                    weigh(n, p - 1, STEPS - 1)
                            elif part[0] == "score":
                                score(n, p, k, part[1])
                            else:
                                h = part[1]
                                max_scores(n, JOB[p, k, "max", h], u // NCH % 2, u % NCH, k, h)
                        for e in extras(p, k):
                            extra(n, p, k, e)
                weigh(n, PERIODS - 1, STEPS - 1)
            outputs_to_tokens(PAIRS, 0, PAIRS * PERIODS + 1)
            outputs_to_features(PAIRS, 1, 0, NCH - 1)
            project_out(PAIRS, 2, 1)

        @block.scalar
        def _(act):
            def take_outputs(n, done, job):
                act.wait_ge(summed, done)
                act.wait_ge(ring_full, job)
                nc.scalar.activation(o_raw[:, :], p_av[:, :], ACT.Copy).then_inc(o_raw_ready, 1)

            def take_levels(c):
                act.wait_ge(level_made, c + 1)
                if c >= 2:
                    act.wait_ge(level_stored[c % 2], 16 * (c // 2))
                    act.wait_ge(turned_made, c - 1)
                nc.scalar.activation(level[:, c % 2, :], p_level[:, c % 2, :], ACT.Copy).then_inc(level_out, 1)
                act.wait_ge(level_out, c + 1)
                act.dma_start(xN_pairs[1 + B:1 + 2 * B, c * T:(c + 1) * T, :].rearrange("b t f -> t b f"),
                              level[:, c % 2, :].rearrange("t (b f) -> t b f", b=B)).then_inc(level_stored[c % 2], 16)

            def take_turned(c):
                q = c // TC
                act.wait_ge(turned_made, c + 1)
                if q >= 2:
                    act.wait_ge(turned_stored[q % 2], 16 * (q // 2))
                nc.scalar.activation(level_T[:, q % 2, :, (c % TC) * T:(c % TC + 1) * T],
                                     p_turned[:, c % 2, :].rearrange("f (b t) -> f b t", b=B), ACT.Copy
                                     ).then_inc(turned_out, 1)
                if c % TC == TC - 1:
                    act.wait_ge(turned_out, c + 1)
                    act.dma_start(xT_pairs[B:2 * B, :, q * C:(q + 1) * C].rearrange("b f t -> f b t"),
                                  level_T[:, q % 2, :, :]).then_inc(turned_stored[q % 2], 16)

            act.wait_ge(ones_set, 4)
            act.wait_ge(parts_ready, NCH)
            stack_rows(act, 1, 0)
            act.wait_ge(parts_ready, 2 * NCH)
            stack_rows(act, 0, 0, range(len(Q_PART) // 2, len(Q_PART)))
            for c in range(NT):
                take_levels(c)
                take_turned(c)
            for i in range(2):
                act.wait_ge(level_stored[i], 16 * NT // 2)
                act.wait_ge(turned_stored[i], 16 * NCH // 2)

            with act.Fori(0, PAIRS) as n:
                for p in range(PERIODS):
                    for k in range(STEPS):
                        for pair in range(2):
                            act.wait_ge(scored, 2 * step_of(n, p, k) + pair + 1)
                            if p or k >= 2:
                                act.wait_ge(summed, step_of(n, p, k) - 1)
                            nc.scalar.activation(prob[k % 2][:, 2 * pair:2 * pair + 2, :], p_exp[pair][:, :, :],
                                                 ACT.Exp, scale=1.0 / DK ** 0.5).then_inc(exped, 1)
                        if k == 0 and p:
                            take_outputs(n, step_of(n, p, 0), ring_of(n, JOB[p - 1, 2, "o_tok"]) + 1)
                take_outputs(n, step_of(n, PERIODS, 0), ring_of(n, JOB[PERIODS - 1, 2, "o_tok"]) + 1)

        @block.vector
        def _(dve):
            def full(n, job):
                dve.wait_ge(ring_full, ring_of(n, job) + 1)
                return p_ring[(R0 + job) % RING]

            def take_max(n, job, par, k, h):
                nc.vector.reduce_max(mpart[par][:, h * TC + k // NCH, k % NCH:k % NCH + 1], full(n, job)[:, :],
                                     AX.X).then_inc(ring_read, 1)

            def combine(n, job, par):
                dve.wait_ge(ring_read, ring_of(n, job))
                nc.vector.tensor_reduce(mneg[:, :], mpart[par][:, :, :], AX.X, ALU.max, negate=True
                                        ).then_inc(max_neg, 1)

            def split_rows(n, job, done):
                bank = full(n, job)
                if not isinstance(done, int) or done:
                    dve.wait_ge(rows_stored, 16 * done)
                nc.vector.tensor_copy(mrow[:, 0, :], bank[0:G * TC, 0:T]).then_inc(max_high, 1)
                dve.wait_ge(max_high, done + 1)
                nc.vector.tensor_tensor(mrow[:, 1, :], bank[0:G * TC, 0:T], mrow[:, 0, :], ALU.subtract
                                        ).then_inc(ring_read, 1)

            def take_qk(n, job, which, i, done):
                bank = full(n, job)
                if not isinstance(done, int) or done >= 2:
                    dve.wait_ge(parts_ready, done - 1)
                nc.vector.tensor_scalar(qk_f[i % 2][:, :], bank[:, :], bqk[:, which:which + 1], None, ALU.add
                                        ).then_inc(ring_read, 1)

            def take_v(n, job, t0, count):
                bank = full(n, job)
                nc.vector.tensor_tensor(vs[:, t0:t0 + count, :], bank[:, 0:count * DH].rearrange("p (t f) -> p t f", f=DH),
                                        bv[:, :].rearrange("p (o f) -> p o f", o=1).broadcast_to([T, count, DH]),
                                        ALU.add).then_inc(ring_read, 1)

            def normalise(n, job, g, c, done):
                bank = full(n, job)[:, :].rearrange("p (t h d) -> p t h d", t=TC, h=G)
                nc.vector.reciprocal(o_rec[:, :, :], bank[:, :, :, DK]).then_inc(o_rec_ready, 1)
                dve.wait_ge(o_rec_ready, done + 1)
                nc.vector.tensor_tensor(
                    o_tok[:, c * TC:(c + 1) * TC, g * G * DK:(g + 1) * G * DK].rearrange("p t (h d) -> p t h d", h=G),
                    bank[:, :, :, 0:DK], o_rec[:, :, :].rearrange("p t (h o) -> p t h o", o=1).broadcast_to([T, TC, G, DK]),
                    ALU.mult).then_inc(ring_read, 1)

            def take_features(n, job):
                nc.vector.tensor_copy(o_feat[:, :], full(n, job)[:, :]).then_inc(ring_read, 1)

            def add_residual(n, job, i, done, stores):
                bank = full(n, job)
                dve.wait_ge(res_ready, done + 3)
                dve.wait_ge(z_stored[i], 16 * stores)
                nc.vector.tensor_tensor(z[i][:, :, :], bank[:, :].rearrange("p (t f) -> p t f", t=TC), res_b[:, :, :],
                                        ALU.add).then_inc(ring_read, 1)

            def split(which, i, c):
                parts = qk_part[which]
                cols = slice(c * C, (c + 1) * C)
                dve.wait_ge(ring_read, i + 1)
                nc.vector.tensor_copy(parts[0][:, cols], qk_f[i % 2][:, :]).then_inc(split_step, 1)
                dve.wait_ge(split_step, 3 * i + 1)
                nc.vector.tensor_tensor(rest[:, :], qk_f[i % 2][:, :], parts[0][:, cols], ALU.subtract
                                        ).then_inc(split_step, 1)
                dve.wait_ge(split_step, 3 * i + 2)
                nc.vector.tensor_copy(parts[1][:, cols], rest[:, :]).then_inc(split_step, 1)
                dve.wait_ge(split_step, 3 * i + 3)
                nc.vector.tensor_tensor(parts[2][:, cols], rest[:, :], parts[1][:, cols], ALU.subtract
                                        ).then_inc(parts_ready, 1)
                dve.wait_ge(parts_ready, i + 1)

            dve.wait_ge(qkv_loaded, 64)
            for i, job in enumerate(RUN_IN):
                if job == ("max", 0, 0, 0):
                    dve.wait_ge(states_summed, 1)
                    nc.vector.tensor_copy(states[:, :], p_states).then_inc(states_set, 1)
                if job[0] == "qk":
                    take_qk(0, i - R0, job[1], i, i)
                    split(job[1], i, job[2])
                elif job[0] == "v":
                    take_v(0, i - R0, job[1], job[2])
                elif job[0] == "max":
                    take_max(0, i - R0, job[1], job[2], job[3])
                else:
                    split_rows(0, i - R0, 0)
                if job == ("max", 0, STEPS - 1, G - 1):
                    combine(0, i + 1 - R0, 0)

            def extra(n, p, k, e):
                job = JOB[(p, k) + e]
                if e[0] == "max_rows":
                    split_rows(n, job, n * PERIODS + p + 1)
                elif e[0] == "o_tok":
                    normalise(n, job, (p - 1) % PERIODS // NCH, (p - 1) % NCH, n * PERIODS + p)
                elif e[0] == "o_feat":
                    take_features(n, job)
                elif e[0] == "project":
                    f = FIN.index(p)
                    add_residual(n, job, f % 2, n * len(FIN) + f, n * 2 + f // 2 + 1)
                elif e[0] == "qk":
                    i = 2 * e[2] + e[1]
                    if i == 0:
                        dve.wait_ge(qkv_loaded, 64 * n + 128)
                    take_qk(n, job, e[1], i, 2 * NCH * n + 2 * NCH + i)
                else:
                    if e[1] == 0:
                        dve.wait_ge(v_copied, 2 * n + 2)
                    take_v(n, job, e[1], e[2])

            with dve.Fori(0, PAIRS) as n:
                for p in range(PERIODS):
                    for k in range(STEPS):
                        if k == 0:
                            combine(n, JOB[p, 0, "max", 0], (p + 1) % 2)
                        for h in range(G):
                            take_max(n, JOB[p, k, "max", h], p % 2, k, h)
                        for e in extras(p, k):
                            extra(n, p, k, e)
            normalise(PAIRS, 0, 1, NCH - 1, PAIRS * PERIODS)
            take_features(PAIRS, 1)
            add_residual(PAIRS, 2, 0, PAIRS * len(FIN), 2 * PAIRS + 1)

        @block.gpsimd
        def _(pool):
            def split(n, job, which, i, c, done):
                parts = qk_part[which]
                cols = slice(c * C, (c + 1) * C)
                pool.wait_ge(ring_read, ring_of(n, job) + 1)
                pool.sem_inc(pool_passed, 1)
                nc.gpsimd.tensor_copy(parts[0][:, cols], qk_f[i % 2][:, :]).then_inc(split_step, 1)
                pool.wait_ge(split_step, 3 * done + 1)
                nc.gpsimd.tensor_tensor(rest[:, :], qk_f[i % 2][:, :], parts[0][:, cols], ALU.subtract
                                        ).then_inc(split_step, 1)
                pool.wait_ge(split_step, 3 * done + 2)
                pool.sem_inc(pool_passed, 1)
                nc.gpsimd.tensor_copy(parts[1][:, cols], rest[:, :]).then_inc(split_step, 1)
                pool.wait_ge(split_step, 3 * done + 3)
                nc.gpsimd.tensor_tensor(parts[2][:, cols], rest[:, :], parts[1][:, cols], ALU.subtract
                                        ).then_inc(parts_ready, 1)
                pool.wait_ge(parts_ready, done + 1)

            def place_values(g, done):
                pool.sem_inc(pool_passed, 1)
                nc.gpsimd.tensor_copy(va[:, :, g * G:(g + 1) * G, 0:DK],
                                      vs[:, :, g * G * DK:(g + 1) * G * DK].rearrange("p t (h d) -> p t h d", h=G)
                                      ).then_inc(v_copied, 1)

            def bias_residual(i, done, loads, last):
                pool.wait_ge(res_loaded, 16 * (done + 1))
                pool.wait_ge(ring_read, last)
                pool.wait_ge(o_loaded, 32 * loads)
                nc.gpsimd.tensor_tensor(res_b[:, :, :], res[i][:, :, :],
                                        bo[:, :].rearrange("p (o f) -> p o f", o=1).broadcast_to([T, TC, DH]), ALU.add
                                        ).then_inc(res_ready, 1)

            fills = [(ks[0][ROWS:ROWS + 2, :, :], 1.0), (ks[1][ROWS:ROWS + 2, :, :], 1.0), (va[:, :, :, :], 1.0),
                     (o_tok[:, :, :], 0.0)]
            for i, (dst, value) in enumerate(fills):
                nc.gpsimd.memset(dst, value).then_inc(ones_set, 1)
                pool.wait_ge(ones_set, i + 1)
            nc.gpsimd.memset(o_raw[:, :], 1.0).then_inc(o_raw_ready, 1)
            pool.wait_ge(o_raw_ready, 1)
            copies = [(xT_pairs[0:B, :, :], x_feat), (xT_pairs[2 * B:2 * B + 1, :, :], x_feat[0:1, :, :]),
                      (xN_pairs[1:1 + B, :, :], x_tok[:, :, 0:DH]), (xN_pairs[0:1, :, :], x_tok[0:1, :, 0:DH])]
            assert len(copies) == COPIES
            for dst, src in copies:
                pool.dma_start(dst, src).then_inc(copied, 16)
            pool.wait_ge(ring_read, 2 * NCH + NT // 4)
            place_values(0, 0)

            def residual_of(n, p):
                f = FIN.index(p)
                before = JOB[FIN[f - 1], 6, "project"] - (JOBS if f == 0 else 0)
                bias_residual(f % 2, n * len(FIN) + f, n + 1 if p == 0 else n + 2, ring_of(n, before) + 1)

            with pool.Fori(0, PAIRS) as n:
                residual_of(n, 0)
                pool.wait_ge(o_raw_ready, n * PERIODS + 1)
                place_values(1, 2 * n + 1)
                pool.wait_ge(stacked, 16 * STACK * (2 * n + 2))
                for p in (2, 3):
                    for k in range(STEPS):
                        for e in extras(p, k):
                            if e[0] == "qk":
                                i = 2 * e[2] + e[1]
                                split(n, JOB[(p, k) + e], e[1], i, e[2], 2 * NCH * n + 2 * NCH + i)
                pool.wait_ge(summed, step_of(n, NCH, 0))
                place_values(0, 2 * n + 2)
                for p in FIN[1:]:
                    residual_of(n, p)
            residual_of(PAIRS, 0)


F32R = mybir.dt.float32r
CHUNKS = B * NCH
DFF, E, TOPK, NG, TOPG, ROUTED_SCALE = 1024, 16, 4, 4, 2, 2.5
EG = E // NG
NF = DFF // 128
NX = E + 2
UNITS = NF + NX
KC = D // 128
CW = 1
FIRST, LOOP_FIRST, LOOP_TURNS = -2, 1, 6
BIG = 3e38

SLOT = dict(f_add=1, f_stats=2, f_scale=2, f_norm=4,
            r_add=8, r_stats=9, r_scale=10, r_norm=10, r_shift=10,
            s_add=11, s_stats=11, s_scale=12, s_norm=12,
            h_turn=14, h_take0=14, h_take1=14, gate=16, gate_take=16, gate_exp=16,
            route_groups=16, route_mask=17, route_experts=20, route_ties=21, route_weights=22, cw_turn=24, cw_take=24,
            z_stats=13, z_scale=18, z_norm=18, z_shift=19, y_turn=20, y_take0=20, y_take1=20, z_bias=22)
FIRST_SLOT = dict(route_groups=0, route_mask=0, route_experts=1, route_ties=1, route_weights=2, cw_turn=6, cw_take=6)
TURNS = [("h", 0), ("h", 1), ("gate", 0), ("y", 0), ("y", 1), ("cw", 0)]
CONSTS = 4
LAG = 2
V_LINKS = 39


class Period:

    def __init__(self, i, turn=None):
        self.i, self.turn = i, turn
        self.prev = i >= 1
        self.experts = i >= 0
        self.next = 0 <= i + 1 < CHUNKS
        self.next2 = i + 2 < CHUNKS
        self.units = (list(range(NF)) if self.next else []) + (list(range(NF, UNITS)) if self.experts else [])
        self.carried = self.prev and self.next
        self.carries = self.experts and self.next2
        self.routes = self.next and i >= 0
        self.jobs = ([("first_cw", 0)] if i == 0 else []) + [
            j for j in TURNS if {"y": self.next2, "cw": self.routes}.get(j[0], self.next)]

    def at(self, table):
        if self.turn is None:
            return table(self.i)
        return self.turn * (table(self.i + 2) - table(self.i)) + table(self.i)

    def num(self, plus=0):
        return self.at(lambda i: i + plus)

    def ring(self, job, j=0):
        return self.at(turns_before) + self.jobs.index((job, j))

    def bank(self, job, j=0):
        return (turns_before(self.i) + self.jobs.index((job, j))) % 2

    def unit(self, u):
        return self.at(units_before) + self.units.index(u)

    def side(self, u):
        return (units_before(self.i) + self.units.index(u)) % 2


def turns_before(i):
    return sum(len(Period(j).jobs) for j in range(FIRST, i))


def units_before(i):
    return sum(len(Period(j).units) for j in range(FIRST, i))


def run_periods(engine, period, chain=None):
    for i in range(FIRST, LOOP_FIRST):
        period(Period(i))
    with engine.Fori(0, LOOP_TURNS) as turn:
        if chain is not None:
            chain.enter(turn)
        for i in range(LOOP_FIRST, LOOP_FIRST + 2):
            period(Period(i, turn))
        if chain is not None:
            chain.leave(LOOP_TURNS)
    for i in range(LOOP_FIRST + 2 * LOOP_TURNS, CHUNKS):
        period(Period(i))


class Count:

    def __init__(self, per_turn):
        self.n, self.per_turn, self.turn, self.start = 0, per_turn, None, 0

    def enter(self, turn):
        self.turn, self.start = turn, self.n

    def leave(self, turns):
        assert self.n - self.start == self.per_turn, (self.n - self.start, self.per_turn)
        self.turn, self.n = None, self.start + turns * self.per_turn

    def next(self):
        self.n += 1
        return self.n if self.turn is None else self.turn * self.per_turn + self.n


def experts(nc, x_tok, z_pairs, ff1, ff2, gate_t, exp_g, exp_u, exp_d, ff_bias1, ff_bias2, affine, gate_bias,
            lower, identity, out):
    x_rows = x_tok.rearrange("b s f -> (b s) f")
    z_rows = z_pairs.rearrange("n s f -> (n s) f")
    out_rows = out.rearrange("b s f -> (b s) f")
    cw_scratch = nc.dram_tensor("cw_scratch", [2, E, C], F32, kind="Internal").ap()
    with ExitStack() as ctx:
        sb = lambda name, shape, dt=F32: ctx.enter_context(nc.sbuf_tensor(name, shape, dt))
        sem = lambda name: ctx.enter_context(nc.semaphore(name))
        w1 = [sb(f"w_ff1_{i}", [128, KC * DFF], F32R) for i in range(2)]
        w2 = [sb(f"w_ff2_{i}", [128, NF * D], F32R) for i in range(2)]
        gw = [sb(f"w_gate{i}", [128, KC * E], F32R) for i in range(2)]
        wg = [sb(f"w_g{i}", [128, NX * D], F32R) for i in range(2)]
        wu = [sb(f"w_u{i}", [128, NX * D], F32R) for i in range(2)]
        wd = [sb(f"w_d{i}", [128, NX * D], F32R) for i in range(2)]
        b1 = sb("bias1", [128, NF])
        b2 = sb("bias2", [T, D])
        aff = sb("affine", [T, 4, D])
        gb = sb("gate_b", [T, E])
        low = sb("lower", [T, E, E])
        low4 = low[:, 0:NG, 0:NG]
        ident = sb("ident2", [128, 128])
        power = sb("power", [T, 2 * TC])
        z = sb("z_in", [T, TC, D])
        yT = [sb(f"y_feat{i}", [128, KC, C], F32R) for i in range(2)]
        x = sb("x_in", [T, TC * D])
        fin = x[:, :].rearrange("p (t f) -> p t f", t=TC)
        h = sb("h_tok", [T, 2, TC, D])
        hT = [[sb(f"h_feat{par}{i}", [128, KC, C], F32R) for i in range(2)] for par in range(2)]
        act_hi = [sb(f"act_hi{i}", [128, C], F32R) for i in range(2)]
        act_lo = [sb(f"act_lo{i}", [128, C], F32R) for i in range(2)]
        gated = [sb(f"gated{i}", [128, C]) for i in range(2)]
        cwb = sb("cw_all", [128, 2, CW, C])
        NORMS = "zrsf"
        stats = {k: sb(f"{k}_stats", [T, 2 * TC, 6]) for k in NORMS}
        mv = {k: sb(f"{k}_mean_var", [T, 2 * TC, 2]) for k in NORMS}
        scale = {k: sb(f"{k}_scale", [T, 2 * TC]) for k in NORMS}
        var_eps = {k: sb(f"{k}_var_eps", [T, 2 * TC]) for k in NORMS}
        logit = sb("logit", [T, TC * E])
        expo = sb("exp_neg", [T, TC * E])
        score = sb("score", [T, TC * E])
        biased = sb("biased", [T, TC * NG, EG])
        pair_sum = sb("pair_sums", [T, TC * NG, 6])
        gscore = sb("group_score", [T, TC, NG])
        gcmp = [sb(f"group_cmp{i}", [T, TC, NG, NG]) for i in range(2)]
        grank = sb("group_rank", [T, TC * NG])
        gpen = sb("group_penalty", [T, TC * NG])
        masked = sb("masked", [T, TC * NG, EG])
        erank = sb("expert_rank", [T, TC * E])
        wsel = sb("w_selected", [T, TC, E])
        wsum = sb("w_sum", [T, TC])
        cw = sb("cw_tok", [T, TC, E])
        cwT = x[0:E, 0:C]
        ecmp = [x[:, k * C:(k + 1) * C].bitcast(BF16).rearrange("p (t i j) -> p t i j", t=TC, i=E) for k in range(2)]

        p_unit = [ctx.enter_context(nc.psum_tensor(f"p_unit{i}", [128, 2, C], F32)) for i in range(2)]
        p_acc = ctx.enter_context(nc.psum_tensor("p_acc", [T, TC, D], F32))
        p_ring = [ctx.enter_context(nc.psum_tensor(f"p_turn{i}", [128, C], F32)) for i in range(2)]

        norm_loaded = sem("norm_loaded")
        const_loaded, raw_loaded = sem("const_loaded"), [sem(f"raw_loaded{i}") for i in range(4)]
        hi_made, lo_made, power_set = sem("w_hi_made"), sem("w_lo_made"), sem("power_set")
        ring_full, ring_read = sem("turn_full"), sem("turn_read")
        up_done, silu_done, weighted, operand = sem("up_done"), sem("silu_done"), sem("weighted"), sem("operand")
        product_made, down_done, r_added, f_added = sem("product_made"), sem("down_done"), sem("r_added"), sem("f_added")
        z_loaded, x_loaded = sem("z_loaded"), sem("x_loaded")
        cw_ready, cw_stored = sem("cw_ready"), sem("cw_stored")
        cw_loaded = [sem(f"cw_loaded{i}") for i in range(2)]
        var_ready = {k: sem(f"{k}_var_ready") for k in NORMS}
        scale_ready = {k: sem(f"{k}_scale_ready") for k in NORMS}
        ff_made, high_made, z_biased = sem("ff_made"), sem("high_made"), sem("z_biased")
        y_ready, h_ready, gate_exped = sem("y_ready"), sem("h_ready"), sem("gate_exped")
        f_ready, f_stored = sem("f_ready"), sem("f_stored")
        v_step = sem("v_step")
        v_passed, s_passed = sem("v_passed"), sem("s_passed")
        block = ctx.enter_context(nc.Block())

        STAGE = TC * D
        pieces = [(src, dst, a, min(STAGE, n - a))
                  for src, dst, n in ((ff1, w1, KC * DFF), (ff2, w2, NF * D), (gate_t, gw, KC * E),
                                      (exp_g, wg, NX * D), (exp_u, wu, NX * D), (exp_d, wd, NX * D))
                  for a in range(0, n, STAGE)]
        FF_PIECES = (KC * DFF + NF * D) // STAGE
        staging = [h[:, k, :, :].rearrange("p t f -> p (t f)") for k in range(2)
                   ] + [cwb[:, :, :, :].rearrange("p a e c -> p (a e c)"), x[:, :]]

        @block.sync
        def _(sp):
            def load_z(c):
                for half in range(2):
                    row = c * C + (1 + B * half) * S
                    sp.dma_start(z[:, :, half * DH:(half + 1) * DH],
                                 z_rows[bass.ds(row, C), :].rearrange("(t p) f -> p t f", p=T)).then_inc(z_loaded, 16)

            def load_x(c):
                row = c * C
                sp.dma_start(x[:, :], x_rows[bass.ds(row, C), :].rearrange("(t p) f -> p t f", p=T)).then_inc(x_loaded, 16)

            def store(c):
                row = c * C
                sp.wait_ge(f_ready, c + 1)
                sp.dma_start(out_rows[bass.ds(row, C), :].rearrange("(t p) f -> p t f", p=T), fin[:, :, :]
                             ).then_inc(f_stored, 16)

            load_z(0)
            for dst, src in ((aff[:, :, :], affine), (ident[:, :], identity)):
                sp.dma_start(dst, src).then_inc(norm_loaded, 16)
            consts = ((b1[:, :], ff_bias1), (b2[:, :], ff_bias2), (gb[:, :], gate_bias), (low[:, :, :], lower))
            assert len(consts) == CONSTS
            for dst, src in consts:
                sp.dma_start(dst, src).then_inc(const_loaded, 16)
            sp.sem_inc(f_stored, 16)
            for k, (src, _, a, n) in enumerate(pieces):
                if k >= 4:
                    sp.wait_ge(lo_made, k - 3)
                sp.dma_start(staging[k % 4][:, 0:n], src[:, a:a + n]).then_inc(raw_loaded[k % 4], 16)

            def store_weights(job, c):
                sp.wait_ge(ring_read, job + 1)
                sp.dma_start(cw_scratch[c % 2, :, :], cwT).then_inc(cw_stored, 16)

            def period(P):
                if P.i == 0:
                    store_weights(P.ring("first_cw"), 0)
                    sp.wait_ge(cw_stored, 16)
                for e in range(0, E, CW):
                    if e == 2 * CW and P.prev:
                        store(P.num(-1))
                    if e == 2 * CW and P.next:
                        if P.i == FIRST + 1:
                            sp.wait_ge(lo_made, len(pieces))
                        if P.prev:
                            sp.wait_ge(f_stored, 16 * P.num(1))
                        load_x(P.num(1))
                    if P.experts:
                        if P.i > 0 or e >= 2 * CW:
                            sp.wait_ge(weighted, P.at(lambda i: i * E) + e - CW)
                        sp.dma_start(cwb[:, e // CW % 2, :, :], cw_scratch[P.i % 2:P.i % 2 + 1, e:e + CW, :].broadcast_to([128, CW, C])
                                     ).then_inc(cw_loaded[e // CW % 2], 16)
                    if e == 3 * CW and P.next2 and P.i > FIRST:
                        sp.wait_ge(r_added, P.num(2))
                        load_z(P.num(2))
                if P.routes:
                    store_weights(P.ring("cw"), P.i + 1)
                    sp.wait_ge(cw_stored, 16 * P.num(2))
                    sp.sem_inc(s_passed, 1)

            run_periods(sp, period)
            store(CHUNKS - 1)
            sp.wait_ge(f_stored, 16 * (CHUNKS + 1))

        @block.tensor
        def _(pe):
            def exact(dst, lhs, rhs, start, stop):
                nc.tensor.matmul(dst, lhs[0], rhs[0], start=start, stop=False)
                nc.tensor.matmul(dst, lhs[0], rhs[1], start=False, stop=False)
                return nc.tensor.matmul(dst, lhs[1], rhs[0], start=False, stop=stop)

            def bank_of(P, job, j=0):
                idx = P.ring(job, j)
                if P.turn is not None or idx >= 2:
                    pe.wait_ge(ring_read, idx - 1)
                return p_ring[P.bank(job, j)]

            def turn_weights(P, job, done):
                pe.wait_ge(cw_ready, done)
                bank = bank_of(P, job)
                for t in range(TC):
                    last = nc.tensor.transpose(bank[0:E, t * T:(t + 1) * T], cw[:, t, :], ident[:, :])
                last.then_inc(ring_full, 1)

            def turn_tokens(P, job, src):
                for j in range(2):
                    bank = bank_of(P, job, j)
                    for t in range(TC):
                        last = nc.tensor.transpose(bank[:, t * T:(t + 1) * T], src[:, t, j * 128:(j + 1) * 128],
                                                   ident[:, :])
                    last.then_inc(ring_full, 1)

            def up(P, u):
                side = P.side(u)
                if P.units.index(u) >= LAG and u - LAG < NF or P.i == 0 and u < LAG:
                    pe.wait_ge(ff_made, P.at(lambda i: (i + 1) * NF) + u - 1)
                elif P.experts:
                    pe.wait_ge(product_made, P.at(lambda i: i * NX) + (u - NF if u >= NF else u) - 1)
                if P.i == FIRST + 1 and u == 0:
                    pe.wait_ge(lo_made, FF_PIECES)
                if u in (0, NF):
                    pe.wait_ge(ring_read, P.at(turns_before))
                if u < NF:
                    for k in range(KC):
                        cols = slice(k * DFF + u * 128, k * DFF + (u + 1) * 128)
                        last = exact(p_unit[side][:, 0, :], [w_[:, cols] for w_ in w1], [p_[:, k, :] for p_ in yT],
                                     k == 0, k == KC - 1)
                else:
                    e = u - NF
                    for i, ws in enumerate((wg, wu)):
                        for k in range(KC):
                            cols = slice(e * D + k * 128, e * D + (k + 1) * 128)
                            last = exact(p_unit[side][:, i, :], [w_[:, cols] for w_ in ws],
                                         [p_[:, k, :] for p_ in hT[P.i % 2]], k == 0, k == KC - 1)
                last.then_inc(up_done, 1)

            def down(P, u):
                side = P.side(u)
                pe.wait_ge(operand, P.unit(u) + 1)
                if u == 0 and P.prev:
                    pe.wait_ge(f_added, P.num())
                if u == NF:
                    if P.next:
                        pe.wait_ge(r_added, P.num(2))
                    else:
                        pe.wait_ge(f_added, P.num())
                ws, e = (w2, u) if u < NF else (wd, u - NF)
                for t in range(TC):
                    last = exact(p_acc[:, t, :], [a_[side][:, t * T:(t + 1) * T] for a_ in (act_hi, act_lo)],
                                 [w_[:, e * D:(e + 1) * D] for w_ in ws], u in (0, NF) and t % 2 == 0,
                                 u in (NF - 1, UNITS - 1) and t % 2 == 1)
                last.then_inc(down_done, 1)

            def steps(P, u):
                if P.next and u == SLOT["h_turn"]:
                    pe.wait_ge(h_ready, P.num(2))
                    turn_tokens(P, "h", h[:, (P.i + 1) % 2, :, :])
                if P.next and u == SLOT["gate"]:
                    if P.i < 0:
                        pe.wait_ge(lo_made, FF_PIECES + 1)
                    pe.wait_ge(ring_read, P.ring("h", 1) + 1)
                    bank = bank_of(P, "gate")
                    for t in range(TC):
                        for k in range(KC):
                            last = exact(bank[:, t * E:(t + 1) * E], [p_[:, k, t * T:(t + 1) * T] for p_ in hT[(P.i + 1) % 2]],
                                         [w_[:, k * E:(k + 1) * E] for w_ in gw], k == 0, k == KC - 1)
                    last.then_inc(ring_full, 1)
                if P.next2 and u == SLOT["y_turn"]:
                    pe.wait_ge(y_ready, P.num(3))
                    turn_tokens(P, "y", z)
                if P.routes and u == SLOT["cw_turn"]:
                    turn_weights(P, "cw", P.num(2))
                if P.i == 0 and u == FIRST_SLOT["cw_turn"]:
                    turn_weights(P, "first_cw", 1)

            def period(P):
                behind = []
                if P.carried:
                    last_period = Period(P.i - 1, P.turn)
                    behind = [(last_period, UNITS - 2), (last_period, UNITS - 1)]
                for u in range(UNITS):
                    if u in P.units:
                        if P.i == 0 and u == NF:
                            pe.wait_ge(lo_made, len(pieces))
                        up(P, u)
                        behind.append((P, u))
                    while len(behind) > (LAG if u in P.units else 0):
                        down(*behind.pop(0))
                    steps(P, u)
                if not P.carries:
                    for unit in behind:
                        down(*unit)

            pe.wait_ge(norm_loaded, 2 * 16)
            run_periods(pe, period)

        @block.scalar
        def _(act):
            def high_parts(k):
                _, dst, a, n = pieces[k]
                act.wait_ge(raw_loaded[k % 4], 16 * (k // 4 + 1))
                nc.scalar.activation(dst[0][:, a:a + n], staging[k % 4][:, 0:n], ACT.Copy).then_inc(hi_made, 1)

            def high_part(P, u):
                side = P.side(u)
                if u >= NF:
                    act.wait_ge(product_made, P.at(lambda i: i * NX) + u - NF + 1)
                else:
                    act.wait_ge(ff_made, P.at(lambda i: (i + 1) * NF) + u + 1)
                if P.i >= 0 or u >= 2:
                    act.wait_ge(down_done, P.unit(u) - 1)
                nc.scalar.activation(act_hi[side][:, :], gated[side][:, :], ACT.Copy).then_inc(high_made, 1)

            def period(P):
                if P.i == FIRST + 1:
                    for k in range(FF_PIECES):
                        high_parts(k)
                for u in range(UNITS):
                    if u in P.units:
                        side = P.side(u)
                        act.wait_ge(up_done, P.unit(u) + 1)
                        if P.i >= 0 or u >= 2:
                            act.wait_ge(operand, P.unit(u) - 1)
                        if u < NF:
                            nc.scalar.activation(gated[side][:, :], p_unit[side][:, 0, :], ACT.Relu, bias=b1[:, u:u + 1]
                                                 ).then_inc(ff_made, 1)
                        else:
                            nc.scalar.activation(gated[side][:, :], p_unit[side][:, 0, :], ACT.Silu
                                                 ).then_inc(silu_done, 1)
                    if u - 1 in P.units:
                        high_part(P, u - 1)
                    if P.i == FIRST + 1 and u < NF:
                        high_parts(FF_PIECES + 2 * u)
                        high_parts(FF_PIECES + 2 * u + 1)
                    if P.next and u == SLOT["gate_exp"]:
                        act.wait_ge(ring_read, P.ring("gate") + 1)
                        nc.scalar.activation(expo[:, :], logit[:, :], ACT.Exp, scale=-1.0).then_inc(gate_exped, 1)
                if P.experts:
                    high_part(P, UNITS - 1)

            act.wait_ge(const_loaded, CONSTS * 16)
            run_periods(act, period)

        @block.vector
        def _(dve):
            count = Count(2 * V_LINKS)

            def link(instruction):
                instruction.then_inc(v_step, 1)
                dve.wait_ge(v_step, count.next())

            def full(P, job, j=0):
                dve.wait_ge(ring_full, P.ring(job, j) + 1)
                return p_ring[P.bank(job, j)]

            def statistics(k, rows):
                n = len(rows)
                for i, row in enumerate(rows):
                    last = nc.vector.bn_stats(stats[k][:, i, :], row)
                link(last)
                dve.sem_inc(v_passed, 1)
                for i in range(n):
                    last = nc.vector.bn_aggr(mv[k][:, i, :], stats[k][:, i, :])
                link(last)
                nc.vector.tensor_scalar(var_eps[k][:, 0:n], mv[k][:, 0:n, 1], EPS, None, ALU.add
                                        ).then_inc(var_ready[k], 1)

            def normalise(k, rows, c):
                dve.wait_ge(scale_ready[k], c + 1)
                for i, row in enumerate(rows):
                    last = nc.vector.tensor_scalar(row, row, mv[k][:, i, 0:1], scale[k][:, i:i + 1],
                                                   ALU.subtract, ALU.mult)
                return last

            def normalise_times(k, rows, factors):
                for i, row in enumerate(rows):
                    last = nc.vector.scalar_tensor_tensor(out=row, in0=row, scalar=mv[k][:, i, 0:1],
                                                          in1=factors[i % len(factors)], op0=ALU.subtract, op1=ALU.mult)
                link(last)

            def scale_and_shift(k, rows, shifts, c):
                dve.wait_ge(scale_ready[k], c + 1)
                for i, row in enumerate(rows):
                    last = nc.vector.scalar_tensor_tensor(out=row, in0=row, scalar=scale[k][:, i:i + 1],
                                                          in1=shifts[i % len(shifts)], op0=ALU.mult, op1=ALU.add)
                return last

            tiles = lambda buf: [buf[:, t, :] for t in range(TC)]
            of_half = lambda j: [aff[:, j, f * DH:(f + 1) * DH] for f in range(2)]
            halves = [z[:, t, f * DH:(f + 1) * DH] for t in range(TC) for f in range(2)]

            def product(P, u):
                side = P.side(u)
                dve.wait_ge(up_done, P.unit(u) + 1)
                if u - NF < E:
                    dve.wait_ge(weighted, P.at(lambda i: i * E) + u - NF + 1)
                else:
                    dve.wait_ge(silu_done, P.at(lambda i: i * NX) + u - NF + 1)
                nc.vector.tensor_tensor(gated[side][:, :], p_unit[side][:, 1, :], gated[side][:, :], ALU.mult
                                        ).then_inc(product_made, 1)

            def low_part(P, u):
                side = P.side(u)
                dve.wait_ge(high_made, P.unit(u) + 1)
                nc.vector.tensor_tensor(act_lo[side][:, :], gated[side][:, :], act_hi[side][:, :].bitcast(F32),
                                        ALU.subtract).then_inc(operand, 1)

            def route_groups():
                link(nc.vector.tensor_scalar(expo[:, :], expo[:, :], 1.0, None, ALU.add))
                link(nc.vector.reciprocal(score[:, :], expo[:, :]))
                link(nc.vector.tensor_tensor(biased[:, :, :].rearrange("p (t g) e -> p t (g e)", t=TC),
                                             score[:, :].rearrange("p (t e) -> p t e", t=TC),
                                             gb[:, :].rearrange("p (o e) -> p o e", o=1).broadcast_to([T, TC, E]), ALU.add))
                for a, b_, at in ((slice(0, 2), slice(2, 4), slice(0, 2)), (slice(0, 3, 2), slice(1, 4, 2), slice(2, 4)),
                                  (slice(0, 1), slice(3, 4), slice(4, 5)), (slice(1, 2), slice(2, 3), slice(5, 6))):
                    last = nc.vector.tensor_tensor(pair_sum[:, :, at], biased[:, :, a], biased[:, :, b_], ALU.add)
                link(last)
                link(nc.vector.reduce_max(gscore[:, :, :].rearrange("p t g -> p (t g)"), pair_sum[:, :, :], AX.X))

            def mask_groups():
                other = gscore[:, :, :].rearrange("p t (o g) -> p t o g", o=1).broadcast_to([T, TC, NG, NG])
                own = gscore[:, :, :].rearrange("p t (g o) -> p t g o", o=1).broadcast_to([T, TC, NG, NG])
                nc.vector.tensor_tensor(gcmp[0][:, :, :, :], other, own, ALU.is_gt)
                link(nc.vector.tensor_tensor(gcmp[1][:, :, :, :], other, own, ALU.is_equal))
                link(nc.vector.tensor_tensor(gcmp[1][:, :, :, :], gcmp[1][:, :, :, :],
                                             low4.rearrange("p (o i) j -> p o i j", o=1).broadcast_to([T, TC, NG, NG]), ALU.mult))
                link(nc.vector.tensor_tensor(gcmp[0][:, :, :, :], gcmp[0][:, :, :, :], gcmp[1][:, :, :, :], ALU.add))
                link(nc.vector.reduce_sum(grank[:, :], gcmp[0][:, :, :, :].rearrange("p t i j -> p (t i) j"), AX.X))
                link(nc.vector.tensor_scalar(grank[:, :], grank[:, :], float(TOPG), None, ALU.is_lt))
                link(nc.vector.tensor_scalar(gpen[:, :], grank[:, :], -1.0, BIG, ALU.add, ALU.mult))
                spread = lambda v: v[:, :].rearrange("p (g o) -> p g o", o=1).broadcast_to([T, TC * NG, EG])
                link(nc.vector.tensor_tensor(masked[:, :, :], biased[:, :, :], spread(grank), ALU.mult))
                link(nc.vector.tensor_tensor(masked[:, :, :], masked[:, :, :], spread(gpen), ALU.add))

            def route_experts():
                m = masked[:, :, :].rearrange("p (t g) e -> p t (g e)", t=TC)
                other = m.rearrange("p t (o e) -> p t o e", o=1).broadcast_to([T, TC, E, E])
                own = m.rearrange("p t (e o) -> p t e o", o=1).broadcast_to([T, TC, E, E])
                nc.vector.tensor_tensor(ecmp[0], other, own, ALU.is_gt)
                link(nc.vector.tensor_tensor(ecmp[1], other, own, ALU.is_equal))

            def route_ties():
                link(nc.vector.tensor_tensor(ecmp[1], ecmp[1],
                                             low[:, :, :].rearrange("p (o i) j -> p o i j", o=1).broadcast_to([T, TC, E, E]), ALU.mult))
                link(nc.vector.tensor_tensor(ecmp[0], ecmp[0], ecmp[1], ALU.add))

            def route_weights():
                link(nc.vector.reduce_sum(erank[:, :], ecmp[0].rearrange("p t i j -> p (t i) j"), AX.X))
                link(nc.vector.tensor_scalar(erank[:, :], erank[:, :], float(TOPK), None, ALU.is_lt))
                link(nc.vector.tensor_tensor(wsel[:, :, :].rearrange("p t e -> p (t e)"), erank[:, :], score[:, :], ALU.mult))
                link(nc.vector.reduce_sum(wsum[:, :], wsel[:, :, :], AX.X))
                link(nc.vector.tensor_scalar(wsum[:, :], wsum[:, :], 1e-20, None, ALU.add))
                link(nc.vector.reciprocal(wsum[:, :], wsum[:, :]))
                link(nc.vector.tensor_tensor(wsel[:, :, :], wsel[:, :, :],
                                             wsum[:, :].rearrange("p (t o) -> p t o", o=1).broadcast_to([T, TC, E]), ALU.mult))
                nc.vector.tensor_scalar(cw[:, :, :], wsel[:, :, :], ROUTED_SCALE, None, ALU.mult).then_inc(cw_ready, 1)

            def take_turned(P, job, j, parts):
                bank = full(P, job, j)
                link(nc.vector.tensor_copy(parts[0][:, j, :], bank[:, :]))
                nc.vector.tensor_tensor(parts[1][:, j, :], bank[:, :], parts[0][:, j, :].bitcast(F32),
                                        ALU.subtract).then_inc(ring_read, 1)

            def steps(P, u):
                hp = (P.i + 1) % 2
                if P.prev and u == SLOT["f_add"]:
                    dve.wait_ge(cw_stored, 16 * P.num(1))
                    add_final(P)
                if P.prev and u == SLOT["f_stats"]:
                    dve.wait_ge(f_added, P.num())
                    statistics("f", tiles(fin))
                if P.prev and u == SLOT["f_norm"]:
                    normalise("f", tiles(fin), P.num(-1)).then_inc(f_ready, 1)
                if P.next and u == SLOT["r_add"]:
                    dve.wait_ge(down_done, P.unit(NF - 1) + 1)
                    dve.wait_ge(z_biased, P.num(2))
                    nc.vector.tensor_tensor(h[:, hp, :, :], p_acc[:, :, :], z[:, :, :], ALU.add).then_inc(r_added, 1)
                if P.next and u == SLOT["r_stats"]:
                    dve.wait_ge(r_added, P.num(2))
                    statistics("r", tiles(h[:, hp, :, :]))
                if P.next and u == SLOT["r_norm"]:
                    normalise_times("r", tiles(h[:, hp, :, :]), [aff[:, 2, :]])
                if P.next and u == SLOT["r_shift"]:
                    link(scale_and_shift("r", tiles(h[:, hp, :, :]), [aff[:, 3, :]], P.num(1)))
                if P.next and u == SLOT["s_add"]:
                    dve.wait_ge(x_loaded, 16 * P.num(2))
                    link(nc.vector.tensor_tensor(h[:, hp, :, :].rearrange("p t f -> p (t f)"), h[:, hp, :, :].rearrange("p t f -> p (t f)"),
                                                 x[:, :], ALU.add))
                if P.next and u == SLOT["s_stats"]:
                    statistics("s", tiles(h[:, hp, :, :]))
                if P.next and u == SLOT["s_norm"]:
                    normalise("s", tiles(h[:, hp, :, :]), P.num(1)).then_inc(h_ready, 1)
                for j in range(2):
                    if P.next and u == SLOT[f"h_take{j}"]:
                        take_turned(P, "h", j, hT[hp])
                if P.next and u == SLOT["gate_take"]:
                    nc.vector.tensor_copy(logit[:, :], full(P, "gate")[:, 0:TC * E]).then_inc(ring_read, 1)
                if P.next2 and u == SLOT["z_stats"]:
                    dve.wait_ge(z_loaded, 32 * P.num(3))
                    statistics("z", halves)
                if P.next2 and u == SLOT["z_norm"]:
                    normalise_times("z", halves, of_half(0))
                if P.next2 and u == SLOT["z_shift"]:
                    scale_and_shift("z", halves, of_half(1), P.num(2)).then_inc(y_ready, 1)
                for j in range(2):
                    if P.next2 and u == SLOT[f"y_take{j}"]:
                        take_turned(P, "y", j, yT)
                if P.routes:
                    route(P, u, SLOT, P.num(2), "cw")
                if P.i == 0:
                    route(P, u, FIRST_SLOT, 1, "first_cw")

            def route(P, u, slot, done, job):
                if u == slot["route_groups"]:
                    dve.wait_ge(gate_exped, done)
                    route_groups()
                if u == slot["route_mask"]:
                    mask_groups()
                if u == slot["route_experts"]:
                    route_experts()
                if u == slot["route_ties"]:
                    route_ties()
                if u == slot["route_weights"]:
                    route_weights()
                if u == slot["cw_take"]:
                    if job == "cw":
                        dve.wait_ge(cw_stored, 16 * P.num(1))
                    nc.vector.tensor_copy(cwT, full(P, job)[0:E, :]).then_inc(ring_read, 1)

            def add_final(P):
                dve.wait_ge(down_done, P.at(units_before))
                nc.vector.scalar_tensor_tensor(out=fin, in0=h[:, (P.i - 1) % 2, :, :], scalar=2.0, in1=p_acc[:, :, :],
                                               op0=ALU.mult, op1=ALU.add).then_inc(f_added, 1)

            def split_weights(k):
                _, dst, a, n = pieces[k]
                dve.wait_ge(hi_made, k + 1)
                nc.vector.tensor_tensor(dst[1][:, a:a + n], staging[k % 4][:, 0:n], dst[0][:, a:a + n].bitcast(F32),
                                        ALU.subtract).then_inc(lo_made, 1)

            def period(P):
                if P.i == FIRST + 1:
                    for k in range(FF_PIECES):
                        split_weights(k)
                for u in range(UNITS):
                    if u - 1 in P.units:
                        low_part(P, u - 1)
                    if u in P.units and u >= NF:
                        product(P, u)
                    if P.i == FIRST + 1 and u < NF:
                        for k in range(FF_PIECES + 2 * u, FF_PIECES + 2 * u + 2):
                            split_weights(k)
                    if P.i == FIRST + 1 and u == NF - 1:
                        dve.wait_ge(lo_made, len(pieces))
                        dve.wait_ge(const_loaded, CONSTS * 16)
                    steps(P, u)
                if P.experts:
                    low_part(P, UNITS - 1)

            dve.wait_ge(norm_loaded, 2 * 16)
            run_periods(dve, period, count)
            dve.wait_ge(f_stored, 16 * CHUNKS)
            add_final(Period(CHUNKS))
            dve.wait_ge(f_added, CHUNKS)
            statistics("f", tiles(fin))
            normalise("f", tiles(fin), CHUNKS - 1).then_inc(f_ready, 1)

        @block.gpsimd
        def _(pool):
            def inverse_root(k, n, c):
                pool.wait_ge(var_ready[k], c + 1)
                nc.gpsimd.tensor_tensor(scale[k][:, 0:n], var_eps[k][:, 0:n], power[:, 0:n], ALU.pow
                                        ).then_inc(scale_ready[k], 1)

            pool.wait_ge(const_loaded, CONSTS * 16)
            nc.gpsimd.memset(power[:, :], -0.5).then_inc(power_set, 1)
            pool.wait_ge(power_set, 1)

            def steps(P, u):
                if P.prev and u == SLOT["f_scale"]:
                    inverse_root("f", TC, P.num(-1))
                if P.next and u == SLOT["r_scale"]:
                    inverse_root("r", TC, P.num(1))
                if P.next and u == SLOT["s_scale"]:
                    inverse_root("s", TC, P.num(1))
                if P.next2 and u == SLOT["z_scale"]:
                    inverse_root("z", 2 * TC, P.num(2))
                if P.next2 and u == SLOT["z_bias"]:
                    pool.wait_ge(ring_read, P.ring("y", 1) + 1)
                    nc.gpsimd.tensor_tensor(z[:, :, :], z[:, :, :], b2[:, :].rearrange("p (o f) -> p o f", o=1).broadcast_to([T, TC, D]),
                                            ALU.add).then_inc(z_biased, 1)

            def period(P):
                for u in range(UNITS):
                    if u in P.units and NF <= u < NF + E:
                        e, side = u - NF, P.side(u)
                        pool.wait_ge(silu_done, P.at(lambda i: i * NX) + e + 1)
                        pool.wait_ge(cw_loaded[e // CW % 2], 16 * (P.at(lambda i: i * E // (2 * CW)) + e // (2 * CW) + 1))
                        nc.gpsimd.tensor_tensor(gated[side][:, :], gated[side][:, :], cwb[:, e // CW % 2, e % CW, :],
                                                ALU.mult).then_inc(weighted, 1)
                    steps(P, u)

            run_periods(pool, period)
            inverse_root("f", TC, CHUNKS - 1)


def build(nc, a, out):
    xT_pairs = nc.dram_tensor("xT_pairs", [PAIRS + 1, DH, S], F32, kind="Internal").ap()
    xN_pairs = nc.dram_tensor("xN_pairs", [PAIRS + 1, S, DH], F32, kind="Internal").ap()
    z_pairs = nc.dram_tensor("z_pairs", [PAIRS + 1, S, DH], F32, kind="Internal").ap()
    attention(nc, a["x_tok"], a["x_feat"], a["holt_in"], a["holt_state"], a["holt_out"], a["holt_carry"], a["x0_rows"],
              a["w_pairs"], a["bias_qk"], a["bias_v"], a["bias_o"], a["identity"], xT_pairs, xN_pairs, z_pairs)
    experts(nc, a["x_tok"], z_pairs, a["ff1"], a["ff2"], a["gate_t"], a["exp_g"], a["exp_u"], a["exp_d"],
            a["ff_bias1"], a["ff_bias2"], a["affine"], a["gate_bias"], a["lower"], a["identity"], out)


def holt_constants():
    import numpy as np

    step = np.array([[1 - ALPHA, 1 - ALPHA], [-ALPHA * BETA, 1 - ALPHA * BETA]])
    gain = np.array([ALPHA, ALPHA * BETA])
    powers = [np.eye(2)]
    for _ in range(S):
        powers.append(powers[-1] @ step)
    levels = np.zeros((T, T))
    for t in range(T):
        for u in range(t + 1):
            levels[u, t] = (powers[t - u] @ gain)[0]
    state_level = np.zeros((2 * NT, NT, T))
    x_state = np.zeros((T, NT, 2 * NT))
    state_state = np.zeros((2, 2 * NT))
    for c in range(NT):
        state_level[2 * c:2 * c + 2, c] = np.stack([powers[t + 1][0] for t in range(T)], 1)
        state_state[:, 2 * c:2 * c + 2] = powers[c * T].T
        for before in range(c):
            x_state[:, before, 2 * c:2 * c + 2] = [powers[(c - before) * T - 1 - u] @ gain for u in range(T)]
    return [a.astype(np.float32) for a in (levels, state_level, x_state, state_state)]


def kernel(**inputs):
    import numpy as np
    import concourse.bacc as bacc
    from concourse.bass_utils import run_bass_kernel_spmd

    f = {k.removeprefix("L0_"): np.asarray(v) for k, v in inputs.items()}
    att = lambda name: f["attn_" + name]
    x = att("x")
    every = lambda v: np.broadcast_to(v, (T,) + v.shape)
    branch = [1] * B + [2] * B + [1]
    half = lambda w: w.reshape(KC, 128, -1).transpose(1, 0, 2)

    def expert_cols(routed, shared):
        w = np.concatenate([routed, shared.reshape(2, 128, D)]).reshape(NX, 128, KC, 128)
        return w.transpose(3, 0, 2, 1).reshape(128, NX * D)

    down = np.concatenate([f["ffn_Wd"], f["ffn_Ws_d"].reshape(D, 2, 128).transpose(1, 0, 2)])
    x0 = np.zeros((2, B, DH), np.float32)
    x0[0] = x[:, 0, :DH]
    levels, state_level, x_state, state_state = holt_constants()
    arrays = {
        "x_tok": x,
        "x_feat": x[:, :, :DH].transpose(0, 2, 1),
        "holt_in": levels, "holt_state": state_level, "holt_out": x_state, "holt_carry": state_state,
        "x0_rows": x0.reshape(2, B * DH),
        "w_pairs": np.stack([np.concatenate([att(f"w{c}{a}").T for c in "qkvo"], 1) for a in branch]),
        "bias_qk": np.stack([np.stack([att(f"bq{a}"), att(f"bk{a}")], 1) for a in branch]),
        "bias_v": np.stack([every(att(f"bv{a}")) for a in branch]),
        "bias_o": np.stack([every(att(f"bo{a}")) for a in branch]),
        "identity": np.eye(128, dtype=np.float32),
        "ff1": half(att("w_ff1").T).reshape(128, KC * DFF),
        "ff2": att("w_ff2").T.reshape(NF, 128, D).transpose(1, 0, 2).reshape(128, NF * D),
        "gate_t": half(f["ffn_gate_w"].T).reshape(128, KC * E),
        "exp_g": expert_cols(f["ffn_Wg"], f["ffn_Ws_g"]),
        "exp_u": expert_cols(f["ffn_Wu"], f["ffn_Ws_u"]),
        "exp_d": down.transpose(2, 0, 1).reshape(128, NX * D),
        "ff_bias1": att("b_ff1").reshape(NF, 128).T,
        "ff_bias2": every(att("b_ff2")),
        "affine": every(np.stack([np.concatenate([att("g1"), att("g2")]), np.concatenate([att("be1"), att("be2")]),
                                  att("g_ff"), att("be_ff")])),
        "gate_bias": every(f["ffn_gate_bias"]),
        "lower": every(np.tril(np.ones((E, E), np.float32), -1)),
    }
    nc = bacc.Bacc("TRN2", target_bir_lowering=False, num_devices=1)
    arrays = {k: np.ascontiguousarray(v) for k, v in arrays.items()}
    ap = {k: nc.dram_tensor("in_" + k, v.shape, mybir.dt.from_np(v.dtype), kind="ExternalInput").ap()
          for k, v in arrays.items()}
    out = nc.dram_tensor("out", (B, S, D), F32, kind="ExternalOutput").ap()
    build(nc, ap, out)
    r = run_bass_kernel_spmd(nc, [{"in_" + k: v for k, v in arrays.items()}], core_ids=[0])
    return r.results[0]["out"]
```
